# Optimizing a Trainium2 kernel written in Bass

```python
import numpy as np
import jax
import jax.numpy as jnp

def _softmax(x, axis=-1):
    return jax.nn.softmax(x, axis=axis)

def _gelu(x):
    return jax.nn.gelu(x, approximate=True)

def _silu(x):
    return jax.nn.silu(x)

def _sigmoid(x):
    return jax.nn.sigmoid(x)

def _layernorm(x, axis=-1, eps=1e-05):
    m = jnp.mean(x, axis=axis, keepdims=True)
    v = jnp.var(x, axis=axis, keepdims=True)
    return (x - m) / jnp.sqrt(v + eps)

def _scatter_add(tgt, idx, src, axis=0):
    return tgt.at[idx].add(src)

def _segment_sum(src, seg, n):
    return jax.ops.segment_sum(src, seg, n)
kernel_name = 'mk_adj_resnorm_d2_adj_r2_7b4fa3'

def setup_inputs(seed: int=0):
    np.random.seed(seed)
    _w = jnp.asarray

    def _rec_inputs():
        import jax
        import jax.numpy as jnp
        _gk = jax.random.key(seed)
        x = 7.22e-05 + 1 * jax.random.normal(jax.random.fold_in(_gk, 1), (128, 128, 256), jnp.float32)
        _a = jax.random.bernoulli(jax.random.fold_in(_gk, 2), 0.03125, (128, 128, 128))
        _a = jnp.logical_or(_a, jnp.swapaxes(_a, -1, -2))
        _a = jnp.logical_or(_a, jnp.eye(128, dtype=bool))
        _af = _a.astype(jnp.float32)
        _af = _af * jax.random.uniform(jax.random.fold_in(_gk, 3), (128, 128, 128), jnp.float32, 0.05, 1)
        adj = _af
        return (x, adj)
    x, adj = _rec_inputs()

    def _L0_gnn_setup():
        import jax, jax.numpy as jnp
        import numpy as np
        EPS_LN = 1e-05

        def hypergraph_conv(x, adj, W, b):
            N, C, _ = adj.shape
            H = (adj != 0).astype(x.dtype)
            w = adj.reshape(N, -1)[:, :C]
            xw = jnp.einsum('ncd,hd->nch', x, W)
            Dn = jnp.einsum('nce,ne->nc', H, w)
            Dn = jnp.where(Dn > 0, 1.0 / Dn, 0.0)
            Be = H.sum(axis=1)
            Be = jnp.where(Be > 0, 1.0 / Be, 0.0)
            m = Be[:, :, None] * jnp.einsum('nce,nch->neh', H, xw)
            out = Dn[:, :, None] * jnp.einsum('nce,neh->nch', H, m)
            return out + b

        def layer_norm(x, g, b):
            mu = jnp.mean(x, axis=-1, keepdims=True)
            var = jnp.var(x, axis=-1, keepdims=True)
            return (x - mu) * jax.lax.rsqrt(var + EPS_LN) * g + b
        key = jax.random.key(seed)
        ks = jax.random.split(key, 4)
        N, C, Din, Dh, Dout = (16, 512, 256, 512, 256)
        x = jax.random.normal(ks[0], (N, C, Din), dtype=jnp.float32)
        adj = jax.random.uniform(ks[1], (N, C, C), dtype=jnp.float32, minval=0.1, maxval=1.0)
        W1 = jax.random.normal(ks[2], (Dh, Din), dtype=jnp.float32) * (1.0 / np.sqrt(Din))
        b1 = jnp.zeros((Dh,), dtype=jnp.float32)
        gamma = jnp.ones((Dh,), dtype=jnp.float32)
        beta = jnp.zeros((Dh,), dtype=jnp.float32)
        W2 = jax.random.normal(ks[3], (Dout, Dh), dtype=jnp.float32) * (1.0 / np.sqrt(Dh))
        b2 = jnp.zeros((Dout,), dtype=jnp.float32)
        return {'x': x, 'adj': adj, 'W1': W1, 'b1': b1, 'gamma': gamma, 'beta': beta, 'W2': W2, 'b2': b2}
    _L0_gnn_all = _L0_gnn_setup()
    _L0_gnn_in = {k: v for k, v in _L0_gnn_all.items() if k in ('W1', 'b1', 'gamma', 'beta', 'W2', 'b2')}
    del _L0_gnn_all

    def _L1_gnn_setup():
        import jax, jax.numpy as jnp
        import numpy as np
        EMBED_DIM = 256
        NUM_HEADS = 8
        HEAD_DIM = EMBED_DIM // NUM_HEADS
        SCALE = HEAD_DIM ** (-0.5)
        B, S = (16, 512)
        key = jax.random.key(seed)
        ks = jax.random.split(key, 12)
        init = lambda k, shape: jax.random.normal(k, shape, dtype=jnp.float32) * EMBED_DIM ** (-0.5)
        return {'x': jax.random.normal(ks[0], (B, S, EMBED_DIM), dtype=jnp.float32), 'adj_matrix': jax.random.uniform(ks[1], (B, S, S), dtype=jnp.float32), 'bond_matrix': jax.random.uniform(ks[2], (B, S, S), dtype=jnp.float32), 'Wq': init(ks[3], (EMBED_DIM, EMBED_DIM)), 'bq': jnp.zeros((EMBED_DIM,), jnp.float32), 'Wk': init(ks[4], (EMBED_DIM, EMBED_DIM)), 'bk': jnp.zeros((EMBED_DIM,), jnp.float32), 'Wv': init(ks[5], (EMBED_DIM, EMBED_DIM)), 'bv': jnp.zeros((EMBED_DIM,), jnp.float32), 'Wo': init(ks[6], (EMBED_DIM, EMBED_DIM)), 'bo': jnp.zeros((EMBED_DIM,), jnp.float32), 'seq_len': S}
    _L1_gnn_all = _L1_gnn_setup()
    _L1_gnn_in = {k: v for k, v in _L1_gnn_all.items() if k in ('Wq', 'bq', 'Wk', 'bk', 'Wv', 'bv', 'Wo', 'bo')}
    del _L1_gnn_all
    return {'x': x, 'adj': adj, 'L0_gnn_W1': _L0_gnn_in['W1'], 'L0_gnn_b1': _L0_gnn_in['b1'], 'L0_gnn_gamma': _L0_gnn_in['gamma'], 'L0_gnn_beta': _L0_gnn_in['beta'], 'L0_gnn_W2': _L0_gnn_in['W2'], 'L0_gnn_b2': _L0_gnn_in['b2'], 'L1_gnn_Wq': _L1_gnn_in['Wq'], 'L1_gnn_bq': _L1_gnn_in['bq'], 'L1_gnn_Wk': _L1_gnn_in['Wk'], 'L1_gnn_bk': _L1_gnn_in['bk'], 'L1_gnn_Wv': _L1_gnn_in['Wv'], 'L1_gnn_bv': _L1_gnn_in['bv'], 'L1_gnn_Wo': _L1_gnn_in['Wo'], 'L1_gnn_bo': _L1_gnn_in['bo']}

def reference(x, adj, L0_gnn_W1, L0_gnn_b1, L0_gnn_gamma, L0_gnn_beta, L0_gnn_W2, L0_gnn_b2, L1_gnn_Wq, L1_gnn_bq, L1_gnn_Wk, L1_gnn_bk, L1_gnn_Wv, L1_gnn_bv, L1_gnn_Wo, L1_gnn_bo):
    import jax
    import jax.numpy as jnp

    def _L0_gnn_ref(x, adj, W1, b1, gamma, beta, W2, b2):
        import jax, jax.numpy as jnp
        import numpy as np
        EPS_LN = 1e-05

        def hypergraph_conv(x, adj, W, b):
            N, C, _ = adj.shape
            H = (adj != 0).astype(x.dtype)
            w = adj.reshape(N, -1)[:, :C]
            xw = jnp.einsum('ncd,hd->nch', x, W)
            Dn = jnp.einsum('nce,ne->nc', H, w)
            Dn = jnp.where(Dn > 0, 1.0 / Dn, 0.0)
            Be = H.sum(axis=1)
            Be = jnp.where(Be > 0, 1.0 / Be, 0.0)
            m = Be[:, :, None] * jnp.einsum('nce,nch->neh', H, xw)
            out = Dn[:, :, None] * jnp.einsum('nce,neh->nch', H, m)
            return out + b

        def layer_norm(x, g, b):
            mu = jnp.mean(x, axis=-1, keepdims=True)
            var = jnp.var(x, axis=-1, keepdims=True)
            return (x - mu) * jax.lax.rsqrt(var + EPS_LN) * g + b
        h = jax.nn.relu(hypergraph_conv(x, adj, W1, b1))
        h = layer_norm(h, gamma, beta)
        y = hypergraph_conv(h, adj, W2, b2)
        return y + x

    def _L1_gnn_ref(x, adj_matrix, bond_matrix, Wq, bq, Wk, bk, Wv, bv, Wo, bo, seq_len):
        import jax, jax.numpy as jnp
        import numpy as np
        EMBED_DIM = 256
        NUM_HEADS = 8
        HEAD_DIM = EMBED_DIM // NUM_HEADS
        SCALE = HEAD_DIM ** (-0.5)
        B, S = (16, 512)
        b = x.shape[0]

        def proj(W, bias):
            y = jnp.einsum('bse,fe->bsf', x, W) + bias
            return y.reshape(b, seq_len, NUM_HEADS, HEAD_DIM).transpose(0, 2, 1, 3)
        q, k, v = (proj(Wq, bq), proj(Wk, bk), proj(Wv, bv))
        scores = jnp.einsum('bhqd,bhkd->bhqk', q, k) * SCALE
        mask = (adj_matrix + bond_matrix)[:, None, :, :]
        scores = scores * mask
        attn = jax.nn.softmax(scores, axis=-1)
        ctx = jnp.einsum('bhqk,bhkd->bhqd', attn, v)
        ctx = ctx.transpose(0, 2, 1, 3).reshape(b, seq_len, EMBED_DIM)
        return jnp.einsum('bse,fe->bsf', ctx, Wo) + bo
    x = _layernorm(x + _L0_gnn_ref(x, adj, L0_gnn_W1, L0_gnn_b1, L0_gnn_gamma, L0_gnn_beta, L0_gnn_W2, L0_gnn_b2), axis=-1)
    x = _layernorm(x + _L1_gnn_ref(x, adj, adj, L1_gnn_Wq, L1_gnn_bq, L1_gnn_Wk, L1_gnn_bk, L1_gnn_Wv, L1_gnn_bv, L1_gnn_Wo, L1_gnn_bo, 128), axis=-1)
    return x

_drawn_inputs = setup_inputs


def setup_inputs(seed=0):
    import zlib

    import numpy as np

    out = dict(_drawn_inputs(seed))
    spreads = {'L0_gnn_b1': (0.0, 0.1),
     'L0_gnn_gamma': (1.0, 0.2),
     'L0_gnn_beta': (0.0, 0.1),
     'L0_gnn_b2': (0.0, 0.1),
     'L1_gnn_bq': (0.0, 0.735),
     'L1_gnn_bk': (0.0, 0.711),
     'L1_gnn_bv': (0.0, 0.1),
     'L1_gnn_bo': (0.0, 0.1)}
    factors = {}
    for name, (base, spread) in spreads.items():
        noise = np.random.default_rng([zlib.crc32(name.encode()), seed]).standard_normal(out[name].shape)
        drawn = base * np.exp(spread * noise) if base else spread * noise
        out[name] = jnp.asarray(drawn.astype(out[name].dtype))
    for name, factor in factors.items():
        out[name] = (out[name] * factor).astype(out[name].dtype)
    return out
```

```python
import concourse.bass as bass
from concourse import mybir
from contextlib import ExitStack

F32 = mybir.dt.float32
F32R = mybir.dt.float32r
BF16 = mybir.dt.bfloat16
ALU = mybir.AluOpType
ACT = mybir.ActivationFunctionType
AX = mybir.AxisListType

EPS = 1e-5
TINY = 1.1754944e-38

CONV_TILES = ["ht", "cols", "dnb", "s", "px0", "px1", "a0", "a1", "a2", "a3",
              "pr0", "pr1", "pr2", "pr3", "o20", "o21"]
ATTN_TILES = ["xt0", "xt1", "q0", "q1", "k0", "k1", "v0", "v1",
              "pt00", "pt01", "pt10", "pt11", "c0", "c1",
              "pt20", "pt21", "pt30", "pt31", "c2", "c3", "ct0", "ct1", "y0", "y1"]
BOTH_TILES = ["xt0", "xt1", "ht", "q0", "q1", "cols", "k0", "k1", "dnb", "s", "v0", "v1",
              "px0", "px1", "a0", "a1", "a2", "a3",
              "pt00", "pt01", "pt10", "pt11", "c0", "c1", "pr0", "pr1", "pr2", "pr3",
              "pt20", "pt21", "pt30", "pt31", "o20", "c2", "c3", "o21", "ct0", "ct1", "y0", "y1"]
RING = 4


class Section:

    def __init__(self, conv, attn, first_use, never_used=False):
        self.conv, self.attn, self.first_use, self.never_used = conv, attn, first_use, never_used
        self.tiles = BOTH_TILES if conv is not None and attn is not None else (
            CONV_TILES if attn is None else ATTN_TILES)

    def bank(self, tile):
        return self.tiles.index(tile) % RING

    def full(self, tile):
        return self.first_use + self.tiles.index(tile) // RING + 1

    def freed(self, tile):
        use = self.tiles.index(tile) // RING
        return None if self.never_used and use == 0 else self.first_use + use


def gnn_kernel(nc, x, adj, w1t, b1, gamma, beta, w2t, b2, wqt, bq, wkt, bk, wvt, bv, wot, bo, out):
    N, C, D = x.shape
    DH = w1t.shape[1]
    HEADS = 8
    HD = D // HEADS
    QSCALE = 2.0 * HD ** -0.5
    G = 4
    GROUPS = N // G
    DT, HT_ = D // C, DH // C
    QT = HEADS // DT
    CONV_USES, ATTN_USES = len(CONV_TILES) // RING, len(ATTN_TILES) // RING
    BOTH_USES = len(BOTH_TILES) // RING

    ctx = ExitStack()
    with ctx:
        def sb(name, shape, dt=F32):
            return ctx.enter_context(nc.sbuf_tensor(name, shape, dt))

        def sem(name):
            return ctx.enter_context(nc.semaphore(name))

        ring = [ctx.enter_context(nc.psum_tensor(f"ring{b}", [128, 512], F32)) for b in range(RING)]
        scores = ctx.enter_context(nc.psum_tensor("scores", [128, QT, 2, DT, C], F32))

        ident_bf = sb("ident_bf", [128, 128], BF16)
        ident = sb("ident", [128, 128])
        ones_bf = sb("ones_bf", [128, 1], BF16)
        ones_r = sb("ones_r", [128, 128], F32R)
        mean_w = sb("mean_w", [128, 128])
        neg_half = sb("neg_half", [128, G])
        stage = sb("stage", [128, 2048])
        W1 = [sb(f"w1_{h}", [128, DT, DH], F32R) for h in ("hi", "lo")]
        W2 = [sb(f"w2_{h}", [128, HT_, D], F32R) for h in ("hi", "lo")]
        WQ = [sb(f"wq_{h}", [128, DT, D], F32R) for h in ("hi", "lo")]
        WK = [sb(f"wk_{h}", [128, DT, D], F32R) for h in ("hi", "lo")]
        WV = [sb(f"wv_{h}", [128, DT, D], F32R) for h in ("hi", "lo")]
        WO = [sb(f"wo_{h}", [128, DT, D], F32R) for h in ("hi", "lo")]
        b1_rows = sb("b1_rows", [128, DH], F32R)
        b1_row = sb("b1_row", [1, DH])
        bias_cols = sb("bias_cols", [128, 4, DT])
        gb_cols = sb("gb_cols", [128, 2, HT_])
        u_rows = sb("u_rows", [128, D])
        b2_rows = sb("b2_rows", [128, D])
        bo_rows = sb("bo_rows", [128, D])
        w_nat = sb("w_nat", [128, C])
        w_rest = sb("w_rest", [128, N])
        w_cols = sb("w_cols", [128, N, 4], BF16)

        x_in = sb("x_in", [128, G, D])
        adj_in = sb("adj_in", [128, G, C])
        H = sb("H", [128, G, C], BF16)
        HT = sb("HT", [128, G, C], BF16)
        wg = sb("wg", [128, G, 4], BF16)
        cd = sb("cd", [128, 2, G])
        rc = sb("rc", [128, G])
        cd_inv = sb("cd_inv", [128, 2, G])
        cd_rec = sb("cd_rec", [128, 2, G])
        cd_rest = sb("cd_rest", [128, 2, G])
        cd_part = sb("cd_part", [128, 3, 2, G], BF16)
        rs = sb("rs", [128, G])
        U = sb("U", [128, 3, G, C], BF16)
        dnb = sb("dnb", [128, G, C])
        PT = sb("PT", [128, G, C])
        PTr = sb("PTr", [128, G, C])
        px = [sb(f"px_{h}", [128, G, DT, C], F32R) for h in ("hi", "lo")]
        r = sb("r", [128, G, DH])
        r_stats = sb("r_stats", [128, G, 6])
        r_mv = sb("r_mv", [128, G, 2])
        r_var = sb("r_var", [128, G])
        r_rstd = sb("r_rstd", [128, G])
        pr = [sb(f"pr_{h}", [128, G, HT_, C], F32R) for h in ("hi", "lo")]
        res1 = sb("res1", [128, G, D])
        res1_b = sb("res1_b", [128, G, D])
        z1 = sb("z1", [128, G, D])
        z1_stats = sb("z1_stats", [128, G, 6])
        z1_mv = sb("z1_mv", [128, G, 2])
        z1_var = sb("z1_var", [128, G])
        z1_rstd = sb("z1_rstd", [128, G])
        x1 = sb("x1", [128, G, D])

        adj_mask = sb("adj_mask", [128, G, C])
        res2 = sb("res2", [128, G, D])
        xt = [sb(f"xt_{h}", [128, DT, G, C], F32R) for h in ("hi", "lo")]
        q = sb("q", [128, DT, G, C])
        k = sb("k", [128, DT, G, C])
        v = sb("v", [128, G, HEADS, HD + 1])
        sm = sb("sm", [128, G, QT, DT, C])
        mx = sb("mx", [128, G, QT, DT])
        pT = sb("pT", [128, 2, HEADS, C])
        rinv = sb("rinv", [128, G, HEADS])
        cx = sb("cx", [128, G, D])
        ct = [sb(f"ct_{h}", [128, DT, G, C], F32R) for h in ("hi", "lo")]
        z2 = sb("z2", [128, G, D])
        z2_stats = sb("z2_stats", [128, G, 6])
        z2_mv = sb("z2_mv", [128, G, 2])
        z2_var = sb("z2_var", [128, G])
        z2_rstd = sb("z2_rstd", [128, G])
        y_out = sb("y_out", [128, G, D])

        bank_full = [sem(f"bank_full{b}") for b in range(RING)]
        bank_free = [sem(f"bank_free{b}") for b in range(RING)]
        scores_full, scores_free = sem("scores_full"), sem("scores_free")
        const_ready, weights_in, weights_ready = sem("const_ready"), sem("weights_in"), sem("weights_ready")
        prep_dve, prep_pe, b1_step = sem("prep_dve"), sem("prep_pe"), sem("b1_step")
        prep_step = sem("prep_step")
        x_loaded, adj_loaded, mask_loaded, stored = sem("x_loaded"), sem("adj_loaded"), sem("mask_loaded"), sem("stored")
        h_ready, ht_ready, wg_ready = sem("h_ready"), sem("ht_ready"), sem("wg_ready")
        cols_step, u_ready, dnb_ready, pt_ready, ptr_ready = (
            sem("cols_step"), sem("u_ready"), sem("dnb_ready"), sem("pt_ready"), sem("ptr_ready"))
        px_hi, px_lo, r_ready, pr_hi, pr_lo = sem("px_hi"), sem("px_lo"), sem("r_ready"), sem("pr_hi"), sem("pr_lo")
        r_read = sem("r_read")
        r_step, r_var_ready, r_rstd_ready = sem("r_step"), sem("r_var_ready"), sem("r_rstd_ready")
        res1_step, z1_step, z1_var_ready, z1_rstd_ready, x1_ready = (
            sem("res1_step"), sem("z1_step"), sem("z1_var_ready"), sem("z1_rstd_ready"), sem("x1_ready"))
        res2_ready, xt_hi, xt_lo = sem("res2_ready"), sem("xt_hi"), sem("xt_lo")
        qk_ready, v_ready = sem("qk_ready"), sem("v_ready")
        sm_ready, mx_ready, sub_ready, p_ready = sem("sm_ready"), sem("mx_ready"), sem("sub_ready"), sem("p_ready")
        rinv_ready, cx_ready, ct_hi, ct_lo = sem("rinv_ready"), sem("cx_ready"), sem("ct_hi"), sem("ct_lo")
        z2_step, z2_var_ready, z2_rstd_ready, y_ready = (
            sem("z2_step"), sem("z2_var_ready"), sem("z2_rstd_ready"), sem("y_ready"))

        x_g = x.rearrange("n c d -> c n d")
        adj_g = adj.rearrange("n c e -> c n e")
        out_g = out.rearrange("n c d -> c n d")
        WEIGHT_LOADS = 15
        COLS_STEPS = 12

        def sections(eng, emit):
            emit(Section(0, None, 0, never_used=True))
            with eng.Fori(0, GROUPS - 1) as j:
                emit(Section(j + 1, j, j * BOTH_USES + CONV_USES))
            emit(Section(None, GROUPS - 1, (GROUPS - 1) * BOTH_USES + CONV_USES))

        block = ctx.enter_context(nc.Block())

        @block.sync
        def _(sp):
            def load(dst, src):
                sp.dma_start(dst, src).then_inc(weights_in, 16)

            X_READ_BANK = CONV_TILES.index("px1") % RING
            assert X_READ_BANK == BOTH_TILES.index("px1") % RING

            sp.dma_start(w_nat[0:N, :], adj[:, 0, :]).then_inc(weights_in, 16)
            sp.dma_start(adj_in[:], adj_g[:, 0:G, :]).then_inc(adj_loaded, 16)
            sp.dma_start(x_in[:], x_g[:, 0:G, :]).then_inc(x_loaded, 16)
            for wt, place in ((w1t, 0), (w2t, 1024)):
                load(stage[:, place:place + 1024].rearrange("p (t n) -> p t n", t=wt.shape[0] // 128),
                     wt.rearrange("(t p) n -> p t n", p=128))
            load(b1_row[:], b1.rearrange("(a n) -> a n", a=1))
            for n, b in enumerate((bq, bk, bv)):
                load(bias_cols[:, n, :], b)
            for n, b in enumerate((gamma, beta)):
                load(gb_cols[:, n, :], b)
            for rows, b in ((b2_rows, b2), (bo_rows, bo)):
                load(rows[:], b.rearrange("(a n) -> a n", a=1).partition_broadcast(128))
            for n, wt in enumerate((wqt, wkt, wvt, wot)):
                load((res2, z2, cx, y_out)[n][:, 0:2, :], wt.rearrange("(t p) n -> p t n", p=128))

            sp.dma_start(adj_mask[:], adj_g[:, 0:G, :]).then_inc(mask_loaded, 16)
            sp.wait_ge(h_ready, 1)
            sp.dma_start(adj_in[:], adj_g[:, G:2 * G, :]).then_inc(adj_loaded, 16)
            sp.wait_ge(bank_full[X_READ_BANK], CONV_TILES.index("px1") // RING + 1)
            sp.wait_ge(res1_step, 3)
            sp.dma_start(x_in[:], x_g[:, G:2 * G, :]).then_inc(x_loaded, 16)
            with sp.Fori(0, GROUPS - 2) as j:
                sp.wait_ge(h_ready, j + 2)
                sp.dma_start(adj_in[:], adj_g[:, bass.ds(j * G + 2 * G, G), :]).then_inc(adj_loaded, 16)
                sp.wait_ge(sm_ready, G * j + G)
                sp.dma_start(adj_mask[:], adj_g[:, bass.ds(j * G + G, G), :]).then_inc(mask_loaded, 16)
                sp.wait_ge(bank_full[X_READ_BANK],
                           j * BOTH_USES + CONV_USES + BOTH_TILES.index("px1") // RING + 1)
                sp.wait_ge(res1_step, 3 * j + 6)
                sp.dma_start(x_in[:], x_g[:, bass.ds(j * G + 2 * G, G), :]).then_inc(x_loaded, 16)
                sp.wait_ge(y_ready, G * j + G)
                sp.dma_start(out_g[:, bass.ds(j * G, G), :], y_out[:]).then_inc(stored, 16)
            sp.wait_ge(sm_ready, G * (GROUPS - 1))
            sp.dma_start(adj_mask[:], adj_g[:, N - G:N, :]).then_inc(mask_loaded, 16)
            for j in (GROUPS - 2, GROUPS - 1):
                sp.wait_ge(y_ready, G * (j + 1))
                sp.dma_start(out_g[:, j * G:(j + 1) * G, :], y_out[:]).then_inc(stored, 16)
            sp.wait_ge(stored, 16 * GROUPS + 16)

        @block.tensor
        def _(pe):
            mm = nc.tensor.matmul

            def claim(s, tile):
                if s.freed(tile) is not None:
                    pe.wait_ge(bank_free[s.bank(tile)], s.freed(tile))
                return ring[s.bank(tile)]

            def split_product(dst, lhs, rhs, extra=None):
                (a_hi, a_lo), (b_hi, b_lo) = lhs, rhs
                n = len(a_hi)
                pairs = [(a_hi[t], b_hi[t]) for t in range(n)] + [(a_hi[t], b_lo[t]) for t in range(n)]
                pairs += [(a_lo[t], b_hi[t]) for t in range(n)]
                if extra:
                    pairs = [extra] + pairs
                for m, (a, b) in enumerate(pairs):
                    last = mm(dst, a, b, start=(m == 0), stop=(m == len(pairs) - 1))
                return last

            pe.wait_ge(const_ready, 8)
            pe.wait_ge(prep_dve, 5)
            w2g = sm[:, 0, 0:QT, :, :].rearrange("p a b c -> p (a b c)")
            nc.tensor.transpose(ring[0][:, 0:N], w_nat[0:N, :], ident[0:N, 0:N]).then_inc(prep_pe, 1)
            for t in range(HT_):
                last = mm(ring[1][:, 0:D], mean_w[:], w2g[:, t * D:(t + 1) * D], start=t == 0, stop=t == HT_ - 1)
            last.then_inc(prep_pe, 1)
            for t in range(HT_):
                last = mm(ring[2][:, 0:D], gb_cols[:, 1, t:t + 1].broadcast_to([128, 128]),
                          stage[:, 1024 + t * D:1024 + (t + 1) * D], start=t == 0, stop=t == HT_ - 1)
            last.then_inc(prep_pe, 1)
            for t in range(DT):
                last = mm(ring[3][:, 0:D], bias_cols[:, 2, t:t + 1].broadcast_to([128, 128]), y_out[:, t, :],
                          start=t == 0, stop=t == DT - 1)
            last.then_inc(prep_pe, 1)
            pe.wait_ge(weights_ready, 1)

            def incidence_transposed(s, i):
                bank = claim(s, "ht")
                pe.wait_ge(h_ready, i + 1)
                dst = bank[:, 0:G * C // 2].bitcast(BF16)
                for g in range(G):
                    last = nc.tensor.transpose(dst[:, g * C:(g + 1) * C], H[:, g, :], ident_bf[:])
                last.then_inc(bank_full[s.bank("ht")], 1)

            def degree_columns(s, i):
                bank = claim(s, "cols")
                pe.wait_ge(ht_ready, i + 1)
                pe.wait_ge(wg_ready, i + 1)
                for g in range(G):
                    mm(bank[:, 8 * g:8 * g + 4], HT[:, g, :], wg[:, g, :], start=True, stop=True)
                    last = mm(bank[:, 8 * g + 4:8 * g + 5], H[:, g, :], ones_bf[:], start=True, stop=True)
                last.then_inc(bank_full[s.bank("cols")], 1)

            def degree_rows(s, i):
                bank = claim(s, "dnb")
                pe.wait_ge(cols_step, COLS_STEPS * i + COLS_STEPS)
                for g in range(G):
                    for m in range(3):
                        last = mm(bank[:, g * C:(g + 1) * C], cd_part[:, m, 1, g:g + 1].broadcast_to([128, 128]),
                                  ident_bf[:], start=m == 0, stop=m == 2)
                last.then_inc(bank_full[s.bank("dnb")], 1)

            def shared_edges(s, i):
                bank = claim(s, "s")
                pe.wait_ge(u_ready, 3 * i + 3)
                for g in range(G):
                    for m in range(3):
                        last = mm(bank[:, g * C:(g + 1) * C], HT[:, g, :], U[:, m, g, :], start=m == 0, stop=m == 2)
                last.then_inc(bank_full[s.bank("s")], 1)

            def propagate_x(s, i, pair):
                tile = f"px{pair}"
                bank = claim(s, tile)
                if pair == 0:
                    pe.wait_ge(pt_ready, i + 1)
                    pe.wait_ge(x_loaded, 16 * i + 16)
                for g in (0, 1):
                    for t in range(DT):
                        at = (g * DT + t) * C
                        last = mm(bank[:, at:at + C], x_in[:, 2 * pair + g, t * C:(t + 1) * C], PT[:, 2 * pair + g, :],
                                  start=True, stop=True)
                last.then_inc(bank_full[s.bank(tile)], 1)

            def hidden(s, i, g):
                tile = f"a{g}"
                bank = claim(s, tile)
                pe.wait_ge(px_lo, 2 * i + g // 2 + 1)
                split_product(bank[:], [[p[:, g, t, :] for t in range(DT)] for p in px],
                              [[w[:, t, :] for t in range(DT)] for w in W1],
                              extra=(ones_r[:], b1_rows[:])).then_inc(bank_full[s.bank(tile)], 1)

            def propagate_r(s, i, g):
                tile = f"pr{g}"
                bank = claim(s, tile)
                if g == 0:
                    pe.wait_ge(ptr_ready, i + 1)
                for t in range(HT_):
                    last = mm(bank[:, t * C:(t + 1) * C], r[:, g, t * C:(t + 1) * C], PTr[:, g, :], start=True, stop=True)
                last.then_inc(bank_full[s.bank(tile)], 1)

            def second_conv(s, i, pair):
                tile = f"o2{pair}"
                bank = claim(s, tile)
                for g in (0, 1):
                    pe.wait_ge(pr_lo, G * i + 2 * pair + g + 1)
                    last = split_product(bank[:, g * D:(g + 1) * D],
                                         [[p[:, 2 * pair + g, t, :] for t in range(HT_)] for p in pr],
                                         [[w[:, t, :] for t in range(HT_)] for w in W2])
                last.then_inc(bank_full[s.bank(tile)], 1)

            def x1_transposed(s, j, t):
                tile = f"xt{t}"
                bank = claim(s, tile)
                if t == 0:
                    pe.wait_ge(x1_ready, G * j + G)
                for g in range(G):
                    last = nc.tensor.transpose(bank[:, g * C:(g + 1) * C], x1[:, g, t * C:(t + 1) * C], ident[:])
                last.then_inc(bank_full[s.bank(tile)], 1)

            def queries_keys(s, j, name, weights, f):
                tile = f"{name}{f}"
                bank = claim(s, tile)
                pe.wait_ge(xt_lo, 2 * j + 2)
                split_product(bank[:], [[w[:, t, f * C:(f + 1) * C] for t in range(DT)] for w in weights],
                              [[a[:, t, :, :].rearrange("p g c -> p (g c)") for t in range(DT)] for a in xt]
                              ).then_inc(bank_full[s.bank(tile)], 1)

            def values(s, j, pair):
                tile = f"v{pair}"
                bank = claim(s, tile)
                for g in (0, 1):
                    last = split_product(bank[:, g * D:(g + 1) * D],
                                         [[a[:, t, 2 * pair + g, :] for t in range(DT)] for a in xt],
                                         [[w[:, t, :] for t in range(DT)] for w in WV])
                last.then_inc(bank_full[s.bank(tile)], 1)

            def score_pair(s, j, pair):
                if pair == 0:
                    pe.wait_ge(qk_ready, 4 * j + 4)
                pe.wait_ge(scores_free, 2 * j + pair + 1)
                for g in (0, 1):
                    for t in range(DT):
                        for h in range(QT):
                            rows = slice(h * HD, (h + 1) * HD)
                            last = mm(scores[:, h, g, t, :], q[rows, t, 2 * pair + g, :], k[rows, t, 2 * pair + g, :],
                                      start=True, stop=True)
                last.then_inc(scores_full, 1)

            def scores_transposed(s, j, g, t):
                tile = f"pt{g}{t}"
                bank = claim(s, tile)
                pe.wait_ge(sub_ready, G * j + g + 1)
                for h in range(QT):
                    last = nc.tensor.transpose(bank[:, h * C:(h + 1) * C], sm[:, g, h, t, :], ident[:])
                last.then_inc(bank_full[s.bank(tile)], 1)

            def context(s, j, g):
                tile = f"c{g}"
                bank = claim(s, tile)
                pe.wait_ge(p_ready, DT * (G * j + g + 1))
                if g == 0:
                    pe.wait_ge(v_ready, 2 * j + 2)
                for h in range(HEADS):
                    last = mm(bank[:, h * (HD + 1):(h + 1) * (HD + 1)], pT[:, g % 2, h, :], v[:, g, h, :],
                              start=True, stop=True)
                last.then_inc(bank_full[s.bank(tile)], 1)

            def context_transposed(s, j, t):
                tile = f"ct{t}"
                bank = claim(s, tile)
                if t == 0:
                    pe.wait_ge(cx_ready, G * j + G)
                for g in range(G):
                    last = nc.tensor.transpose(bank[:, g * C:(g + 1) * C], cx[:, g, t * C:(t + 1) * C], ident[:])
                last.then_inc(bank_full[s.bank(tile)], 1)

            def output(s, j, pair):
                tile = f"y{pair}"
                bank = claim(s, tile)
                if pair == 0:
                    pe.wait_ge(ct_lo, 2 * j + 2)
                for g in (0, 1):
                    last = split_product(bank[:, g * D:(g + 1) * D],
                                         [[a[:, t, 2 * pair + g, :] for t in range(DT)] for a in ct],
                                         [[w[:, t, :] for t in range(DT)] for w in WO])
                last.then_inc(bank_full[s.bank(tile)], 1)

            def emit(s):
                i, j = s.conv, s.attn
                conv, attn = i is not None, j is not None
                if attn:
                    x1_transposed(s, j, 0)
                    x1_transposed(s, j, 1)
                if conv:
                    incidence_transposed(s, i)
                if attn:
                    queries_keys(s, j, "q", WQ, 0)
                    queries_keys(s, j, "q", WQ, 1)
                if conv:
                    degree_columns(s, i)
                if attn:
                    queries_keys(s, j, "k", WK, 0)
                    queries_keys(s, j, "k", WK, 1)
                if conv:
                    degree_rows(s, i)
                    shared_edges(s, i)
                if attn:
                    values(s, j, 0)
                    score_pair(s, j, 0)
                    values(s, j, 1)
                if conv:
                    propagate_x(s, i, 0)
                    propagate_x(s, i, 1)
                    hidden(s, i, 0)
                    hidden(s, i, 1)
                if attn:
                    score_pair(s, j, 1)
                if conv:
                    hidden(s, i, 2)
                    hidden(s, i, 3)
                if attn:
                    for g in (0, 1):
                        scores_transposed(s, j, g, 0)
                        scores_transposed(s, j, g, 1)
                    context(s, j, 0)
                    context(s, j, 1)
                if conv:
                    for g in range(G):
                        propagate_r(s, i, g)
                if attn:
                    for g in (2, 3):
                        scores_transposed(s, j, g, 0)
                        scores_transposed(s, j, g, 1)
                if conv:
                    second_conv(s, i, 0)
                if attn:
                    context(s, j, 2)
                    context(s, j, 3)
                if conv:
                    second_conv(s, i, 1)
                if attn:
                    context_transposed(s, j, 0)
                    context_transposed(s, j, 1)
                    output(s, j, 0)
                    output(s, j, 1)

            sections(pe, emit)

        @block.scalar
        def _(act):
            def filled(s, tile):
                act.wait_ge(bank_full[s.bank(tile)], s.full(tile))
                return ring[s.bank(tile)]

            act.wait_ge(weights_ready, 1)

            def copy(dst, src):
                return nc.scalar.activation(dst, src, ACT.Copy)

            def incidence_transposed(s, i):
                bank = filled(s, "ht")
                copy(HT[:].rearrange("p g c -> p (g c)"), bank[:, 0:G * C // 2].bitcast(BF16)).then_inc(ht_ready, 1)
                act.wait_ge(ht_ready, i + 1)
                act.sem_inc(bank_free[s.bank("ht")], 1)

            def degree_rows(s, i):
                bank = filled(s, "dnb")
                copy(dnb[:].rearrange("p g c -> p (g c)"), bank[:]).then_inc(dnb_ready, 1)
                act.wait_ge(dnb_ready, i + 1)
                act.sem_inc(bank_free[s.bank("dnb")], 1)

            def px_high(s, i, pair):
                bank = filled(s, f"px{pair}")
                copy(px[0][:, 2 * pair:2 * pair + 2, :, :].rearrange("p g t c -> p (g t c)"), bank[:]).then_inc(px_hi, 1)

            def relu(s, i, g):
                bank = filled(s, f"a{g}")
                if g == 0 and not s.never_used:
                    act.wait_ge(r_read, G * i)
                nc.scalar.activation(r[:, g, :], bank[:], ACT.Relu).then_inc(r_ready, 1)
                act.wait_ge(r_ready, G * i + g + 1)
                act.sem_inc(bank_free[s.bank(f"a{g}")], 1)

            def pr_high(s, i, g):
                bank = filled(s, f"pr{g}")
                copy(pr[0][:, g, :, :].rearrange("p t c -> p (t c)"), bank[:]).then_inc(pr_hi, 1)

            def xt_high(s, j, t):
                bank = filled(s, f"xt{t}")
                copy(xt[0][:, t, :, :].rearrange("p g c -> p (g c)"), bank[:]).then_inc(xt_hi, 1)

            def queries_keys(s, j, name, dst, bias, f, n):
                bank = filled(s, f"{name}{f}")
                nc.scalar.activation(dst[:, f, :, :].rearrange("p g c -> p (g c)"), bank[:], ACT.Identity,
                                     bias=bias_cols[:, bias, f:f + 1]).then_inc(qk_ready, 1)
                act.wait_ge(qk_ready, 4 * j + n)
                act.sem_inc(bank_free[s.bank(f"{name}{f}")], 1)

            def values(s, j, pair):
                bank = filled(s, f"v{pair}")
                copy(v[:, 2 * pair:2 * pair + 2, :, 0:HD],
                     bank[:].rearrange("p (g h d) -> p g h d", g=2, h=HEADS)).then_inc(v_ready, 1)
                act.wait_ge(v_ready, 2 * j + pair + 1)
                act.sem_inc(bank_free[s.bank(f"v{pair}")], 1)

            def exponential(s, j, g, t):
                bank = filled(s, f"pt{g}{t}")
                nc.scalar.activation(pT[:, g % 2, t * QT:(t + 1) * QT, :].rearrange("p h c -> p (h c)"), bank[:],
                                     ACT.Exp).then_inc(p_ready, 1)
                act.wait_ge(p_ready, DT * (G * j + g) + t + 1)
                act.sem_inc(bank_free[s.bank(f"pt{g}{t}")], 1)

            def ct_high(s, j, t):
                bank = filled(s, f"ct{t}")
                copy(ct[0][:, t, :, :].rearrange("p g c -> p (g c)"), bank[:]).then_inc(ct_hi, 1)

            def emit(s):
                i, j = s.conv, s.attn
                conv, attn = i is not None, j is not None
                if attn:
                    xt_high(s, j, 0)
                    xt_high(s, j, 1)
                if conv:
                    incidence_transposed(s, i)
                if attn:
                    queries_keys(s, j, "q", q, 0, 0, 1)
                    queries_keys(s, j, "q", q, 0, 1, 2)
                    queries_keys(s, j, "k", k, 1, 0, 3)
                    queries_keys(s, j, "k", k, 1, 1, 4)
                if conv:
                    degree_rows(s, i)
                if attn:
                    values(s, j, 0)
                    values(s, j, 1)
                if conv:
                    px_high(s, i, 0)
                    px_high(s, i, 1)
                    for g in range(G):
                        relu(s, i, g)
                if attn:
                    for g in (0, 1):
                        exponential(s, j, g, 0)
                        exponential(s, j, g, 1)
                if conv:
                    for g in range(G):
                        pr_high(s, i, g)
                if attn:
                    act.wait_ge(bank_full[s.bank("c1")], s.full("c1"))
                    for g in (2, 3):
                        exponential(s, j, g, 0)
                        exponential(s, j, g, 1)
                    ct_high(s, j, 0)
                    ct_high(s, j, 1)

            sections(act, emit)



        @block.vector
        def _(dve):
            V = nc.vector

            def filled(s, tile):
                dve.wait_ge(bank_full[s.bank(tile)], s.full(tile))
                return ring[s.bank(tile)]

            V.memset(b1_rows[:].bitcast(F32), 0.0).then_inc(prep_dve, 1)
            dve.wait_ge(weights_in, 16 * WEIGHT_LOADS)
            dve.wait_ge(prep_dve, 1)
            V.tensor_copy(b1_rows[0:1, :], b1_row[:]).then_inc(b1_step, 1)
            dve.wait_ge(b1_step, 1)
            V.tensor_tensor(b1_rows[32:33, :], b1_row[:], b1_rows[0:1, :].bitcast(F32), ALU.subtract).then_inc(prep_dve, 1)
            count = [0]

            def step(ins):
                count[0] += 1
                ins.then_inc(prep_step, 1)
                dve.wait_ge(prep_step, count[0])

            def split(hi, lo, src):
                step(V.tensor_copy(hi, src))
                step(V.tensor_tensor(lo, src, hi.bitcast(F32), ALU.subtract))

            w2_in = stage[:, 1024:2048].rearrange("p (t n) -> p t n", t=HT_)
            w2g = sm[:, 0, 0:QT, :, :].rearrange("p a b c -> p (a b c)").rearrange("p (t n) -> p t n", t=HT_)
            for t in range(HT_):
                step(V.tensor_scalar(w2g[:, t, :], w2_in[:, t, :], gb_cols[:, 0, t:t + 1], None, ALU.mult))
            step(V.memset(w_cols[:], 1.0))
            step(V.memset(v[:], 1.0))
            dve.sem_inc(prep_dve, 3)
            step(V.tensor_scalar(res2[:, 0:2, :], res2[:, 0:2, :], QSCALE, None, ALU.mult))
            step(V.tensor_scalar(bias_cols[:, 0, :], bias_cols[:, 0, :], QSCALE, None, ALU.mult))
            split(W1[0][:].rearrange("p t n -> p (t n)"), W1[1][:].rearrange("p t n -> p (t n)"), stage[:, 0:1024])
            for w, src in ((WQ, res2), (WK, z2), (WV, cx), (WO, y_out)):
                split(w[0][:], w[1][:], src[:, 0:2, :])
            dve.wait_ge(prep_pe, 1)
            step(V.tensor_copy(w_cols[:, :, 0], ring[0][:, 0:N]))
            step(V.tensor_tensor(w_rest[:], ring[0][:, 0:N], w_cols[:, :, 0], ALU.subtract))
            step(V.tensor_copy(w_cols[:, :, 1], w_rest[:]))
            step(V.tensor_tensor(w_cols[:, :, 2], w_rest[:], w_cols[:, :, 1], ALU.subtract))
            dve.wait_ge(prep_pe, 2)
            for t in range(HT_):
                step(V.tensor_tensor(w2g[:, t, :], w2g[:, t, :], ring[1][:, 0:D], ALU.subtract))
            split(W2[0][:], W2[1][:], w2g)
            dve.wait_ge(prep_pe, 3)
            step(V.tensor_copy(u_rows[:], ring[2][:, 0:D]))
            dve.wait_ge(prep_pe, 4)
            step(V.tensor_tensor(bo_rows[:], bo_rows[:], ring[3][:, 0:D], ALU.add))
            dve.sem_inc(weights_ready, 1)

            def incidence(s, i):
                dve.wait_ge(adj_loaded, 16 * i + 16)
                V.tensor_scalar(H[:], adj_in[:], 0.0, None, ALU.not_equal).then_inc(h_ready, 1)
                V.tensor_copy(wg[:], w_cols[:, bass.ds(i * G, G), :]).then_inc(wg_ready, 1)

            def degrees(s, i):
                bank = filled(s, "cols")
                cols = bank[:, 0:8 * G].rearrange("p (g m) -> p g m", m=8)
                n = [0]

                def link(ins):
                    n[0] += 1
                    ins.then_inc(cols_step, 1)
                    dve.wait_ge(cols_step, COLS_STEPS * i + n[0])

                V.tensor_copy(cd[:, 0, :], cols[:, :, 4]).then_inc(cols_step, 1)
                V.tensor_copy(rc[:], cols[:, :, 3]).then_inc(cols_step, 1)
                n[0] = 2
                link(V.tensor_reduce(cd[:, 1, :], cols[:, :, 0:3], AX.X, ALU.add))
                dve.sem_inc(bank_free[s.bank("cols")], 1)
                link(V.tensor_scalar(cd_inv[:], cd[:], TINY, None, ALU.max))
                link(V.reciprocal(cd_rest[:], cd_inv[:]))
                link(V.scalar_tensor_tensor(out=cd_rec[:], in0=cd[:], scalar=0.0, in1=cd_rest[:],
                                            op0=ALU.is_gt, op1=ALU.mult))
                link(V.tensor_copy(cd_part[:, 0, :, :], cd_rec[:]))
                link(V.tensor_tensor(cd_inv[:], cd_rec[:], cd_part[:, 0, :, :], ALU.subtract))
                link(V.tensor_copy(cd_part[:, 1, :, :], cd_inv[:]))
                link(V.tensor_tensor(cd_rest[:], cd_inv[:], cd_part[:, 1, :, :], ALU.subtract))
                link(V.tensor_copy(cd_part[:, 2, :, :], cd_rest[:]))
                link(V.tensor_tensor(rs[:], cd_rec[:, 1, :], rc[:], ALU.mult))
                assert n[0] == COLS_STEPS
                for m in range(3):
                    V.tensor_tensor(U[:, m, :, :], HT[:],
                                    cd_part[:, m, 0, :].unsqueeze(2).broadcast_to([128, G, C]), ALU.mult).then_inc(u_ready, 1)

            def propagator(s, i):
                bank = filled(s, "s")
                dve.wait_ge(dnb_ready, i + 1)
                V.tensor_tensor(PT[:].rearrange("p g c -> p (g c)"), bank[:],
                                dnb[:].rearrange("p g c -> p (g c)"), ALU.mult).then_inc(pt_ready, 1)
                dve.wait_ge(pt_ready, i + 1)
                dve.sem_inc(bank_free[s.bank("s")], 1)

            def low_half(s, tile, halves, hi_sem, lo_sem, value):
                bank = ring[s.bank(tile)]
                dve.wait_ge(hi_sem, value)
                V.tensor_tensor(halves[1], bank[:], halves[0].bitcast(F32), ALU.subtract).then_inc(lo_sem, 1)
                dve.wait_ge(lo_sem, value)
                dve.sem_inc(bank_free[s.bank(tile)], 1)

            def px_low(s, i, pair):
                low_half(s, f"px{pair}", [p[:, 2 * pair:2 * pair + 2, :, :].rearrange("p g t c -> p (g t c)") for p in px],
                         px_hi, px_lo, 2 * i + pair + 1)

            def hidden_stats(s, i, g):
                dve.wait_ge(r_ready, G * i + g + 1)
                V.bn_stats(r_stats[:, g, :], r[:, g, :]).then_inc(r_step, 1)
                dve.wait_ge(r_step, 2 * G * i + 2 * g + 1)
                dve.sem_inc(r_read, 1)
                V.bn_aggr(r_mv[:, g, :], r_stats[:, g, :]).then_inc(r_step, 1)

            def hidden_scale(s, i):
                dve.wait_ge(r_step, 2 * G * i + 2 * G)
                V.tensor_scalar(r_var[:], r_mv[:, :, 1], EPS, None, ALU.add).then_inc(r_var_ready, 1)

            def scaled_propagator(s, i):
                dve.wait_ge(r_rstd_ready, i + 1)
                V.tensor_tensor(PTr[:], PT[:], r_rstd[:].unsqueeze(2).broadcast_to([128, G, C]),
                                ALU.mult).then_inc(ptr_ready, 1)

            def pr_low(s, i, g):
                low_half(s, f"pr{g}", [p[:, g, :, :].rearrange("p t c -> p (t c)") for p in pr], pr_hi, pr_lo, G * i + g + 1)

            def norm_stats(n, tile, s, pair, z, res, res_sem, res_value, stats, mv, var, z_step, var_ready):
                bank = filled(s, tile)
                dve.wait_ge(res_sem, res_value)
                two = slice(2 * pair, 2 * pair + 2)
                base = 10 * n + 5 * pair
                V.tensor_tensor(z[:, two, :].rearrange("p g d -> p (g d)"), bank[:],
                                res[:, two, :].rearrange("p g d -> p (g d)"), ALU.add).then_inc(z_step, 1)
                dve.wait_ge(z_step, base + 1)
                for g in (0, 1):
                    V.bn_stats(stats[:, 2 * pair + g, :], z[:, 2 * pair + g, :]).then_inc(z_step, 1)
                dve.wait_ge(z_step, base + 3)
                dve.sem_inc(bank_free[s.bank(tile)], 1)
                for g in (0, 1):
                    V.bn_aggr(mv[:, 2 * pair + g, :], stats[:, 2 * pair + g, :]).then_inc(z_step, 1)
                dve.wait_ge(z_step, base + 5)
                V.tensor_scalar(var[:, two], mv[:, two, 1], EPS, None, ALU.add).then_inc(var_ready, 1)

            def normalise(n, pair, dst, z, mv, rstd, rstd_ready, ready):
                dve.wait_ge(rstd_ready, 2 * n + pair + 1)
                for g in (2 * pair, 2 * pair + 1):
                    V.tensor_scalar(dst[:, g, :], z[:, g, :], mv[:, g, 0:1], rstd[:, g:g + 1],
                                    ALU.subtract, ALU.mult).then_inc(ready, 1)

            def xt_low(s, j, t):
                low_half(s, f"xt{t}", [a[:, t, :, :].rearrange("p g c -> p (g c)") for a in xt], xt_hi, xt_lo, 2 * j + t + 1)

            def mask_scores(s, j, pair):
                dve.wait_ge(scores_full, 2 * j + pair + 1)
                if pair == 0:
                    dve.wait_ge(mask_loaded, 16 * j + 16)
                for g in (0, 1):
                    V.tensor_tensor(sm[:, 2 * pair + g, :, :, :], scores[:, :, g, :, :],
                                    adj_mask[:, 2 * pair + g, :].unsqueeze(1).unsqueeze(1).broadcast_to([128, QT, DT, C]),
                                    ALU.mult).then_inc(sm_ready, 1)
                dve.wait_ge(sm_ready, G * j + 2 * pair + 2)
                dve.sem_inc(scores_free, 1)

            def row_max(s, j, g):
                V.tensor_reduce(mx[:, g, :, :], sm[:, g, :, :, :], AX.X, ALU.max).then_inc(mx_ready, 1)

            def context(s, j, g):
                bank = filled(s, f"c{g}")
                heads = bank[:, 0:HEADS * (HD + 1)].rearrange("p (h d) -> p h d", h=HEADS)
                V.reciprocal(rinv[:, g, :], heads[:, :, HD]).then_inc(rinv_ready, 1)
                dve.wait_ge(rinv_ready, G * j + g + 1)
                V.tensor_tensor(cx[:, g, :].rearrange("p (h d) -> p h d", h=HEADS), heads[:, :, 0:HD],
                                rinv[:, g, :].unsqueeze(2).broadcast_to([128, HEADS, HD]), ALU.mult).then_inc(cx_ready, 1)
                dve.wait_ge(cx_ready, G * j + g + 1)
                dve.sem_inc(bank_free[s.bank(f"c{g}")], 1)

            def ct_low(s, j, t):
                low_half(s, f"ct{t}", [a[:, t, :, :].rearrange("p g c -> p (g c)") for a in ct], ct_hi, ct_lo, 2 * j + t + 1)

            def emit(s):
                i, j = s.conv, s.attn
                conv, attn = i is not None, j is not None
                if attn:
                    xt_low(s, j, 0)
                    xt_low(s, j, 1)
                if conv:
                    incidence(s, i)
                    degrees(s, i)
                    propagator(s, i)
                if attn:
                    mask_scores(s, j, 0)
                if conv:
                    px_low(s, i, 0)
                    px_low(s, i, 1)
                if attn:
                    row_max(s, j, 0)
                    row_max(s, j, 1)
                if conv:
                    hidden_stats(s, i, 0)
                    hidden_stats(s, i, 1)
                if attn:
                    mask_scores(s, j, 1)
                if conv:
                    hidden_stats(s, i, 2)
                    hidden_stats(s, i, 3)
                    hidden_scale(s, i)
                if attn:
                    row_max(s, j, 2)
                if conv:
                    scaled_propagator(s, i)
                if attn:
                    row_max(s, j, 3)
                    context(s, j, 0)
                    context(s, j, 1)
                if conv:
                    for g in range(G):
                        pr_low(s, i, g)
                    norm_stats(i, "o20", s, 0, z1, res1, res1_step, 3 * i + 3, z1_stats, z1_mv, z1_var, z1_step, z1_var_ready)
                if attn:
                    context(s, j, 2)
                    context(s, j, 3)
                if conv:
                    normalise(i, 0, x1, z1, z1_mv, z1_rstd, z1_rstd_ready, x1_ready)
                    norm_stats(i, "o21", s, 1, z1, res1, res1_step, 3 * i + 3, z1_stats, z1_mv, z1_var, z1_step, z1_var_ready)
                if attn:
                    ct_low(s, j, 0)
                    ct_low(s, j, 1)
                if conv:
                    normalise(i, 1, x1, z1, z1_mv, z1_rstd, z1_rstd_ready, x1_ready)
                if attn:
                    norm_stats(j, "y0", s, 0, z2, res2, res2_ready, j + 1, z2_stats, z2_mv, z2_var, z2_step, z2_var_ready)
                    norm_stats(j, "y1", s, 1, z2, res2, res2_ready, j + 1, z2_stats, z2_mv, z2_var, z2_step, z2_var_ready)
                    dve.wait_ge(stored, 16 * j + 16)
                    normalise(j, 0, y_out, z2, z2_mv, z2_rstd, z2_rstd_ready, y_ready)
                    normalise(j, 1, y_out, z2, z2_mv, z2_rstd, z2_rstd_ready, y_ready)

            sections(dve, emit)

        @block.gpsimd
        def _(pool):
            P = nc.gpsimd
            P.memset(ident_bf[:], 0.0).then_inc(const_ready, 1)
            P.memset(ident[:], 0.0).then_inc(const_ready, 1)
            P.memset(ones_bf[:], 1.0).then_inc(const_ready, 1)
            P.memset(ones_r[:].bitcast(F32), 1.0).then_inc(const_ready, 1)
            P.memset(mean_w[:], 1.0 / DH).then_inc(const_ready, 1)
            P.memset(neg_half[:], -0.5).then_inc(const_ready, 1)
            pool.wait_ge(const_ready, 6)
            for m in (ident_bf, ident):
                P.affine_select(out=m[:], in_=m[:], compare_op=ALU.not_equal, fill=1.0, base=0,
                                pattern=[[-1, 128]], channel_multiplier=1).then_inc(const_ready, 1)
            pool.sem_inc(scores_free, 1)
            pool.sem_inc(stored, 16)
            pool.wait_ge(weights_ready, 1)

            def inverse_root(rstd, var, ready):
                P.tensor_tensor(rstd, var, neg_half[:, 0:var.shape[1]], ALU.pow).then_inc(ready, 1)

            def residual1(s, i):
                pool.wait_ge(x_loaded, 16 * i + 16)
                P.tensor_tensor(res1_b[:], x_in[:], x_in[:], ALU.add).then_inc(res1_step, 1)
                pool.wait_ge(cols_step, COLS_STEPS * i + COLS_STEPS)
                pool.wait_ge(res1_step, 3 * i + 1)
                P.tensor_tensor(res1_b[:], res1_b[:], b2_rows[:].unsqueeze(1).broadcast_to([128, G, D]), ALU.add)
                for g in range(G):
                    last = P.tensor_scalar(res1[:, g, :], u_rows[:], rs[:, g:g + 1], 0.0, ALU.mult, ALU.add)
                last.then_inc(res1_step, 1)
                pool.wait_ge(res1_step, 3 * i + 2)
                P.tensor_tensor(res1[:], res1[:], res1_b[:], ALU.add).then_inc(res1_step, 1)

            def residual2(s, j):
                pool.wait_ge(x1_ready, G * j + G)
                P.tensor_tensor(res2[:], x1[:], bo_rows[:].unsqueeze(1).broadcast_to([128, G, D]),
                                ALU.add).then_inc(res2_ready, 1)

            def subtract_max(s, j, g):
                pool.wait_ge(mx_ready, G * j + g + 1)
                P.tensor_tensor(sm[:, g, :, :, :], sm[:, g, :, :, :],
                                mx[:, g, :, :].unsqueeze(3).broadcast_to([128, QT, DT, C]), ALU.subtract).then_inc(sub_ready, 1)

            def emit(s):
                i, j = s.conv, s.attn
                conv, attn = i is not None, j is not None
                if attn:
                    residual2(s, j)
                if conv:
                    residual1(s, i)
                if attn:
                    subtract_max(s, j, 0)
                    subtract_max(s, j, 1)
                if conv:
                    pool.wait_ge(r_var_ready, i + 1)
                    inverse_root(r_rstd[:], r_var[:], r_rstd_ready)
                if attn:
                    subtract_max(s, j, 2)
                    subtract_max(s, j, 3)
                for pair in (0, 1):
                    if conv:
                        pool.wait_ge(z1_var_ready, 2 * i + pair + 1)
                        inverse_root(z1_rstd[:, 2 * pair:2 * pair + 2], z1_var[:, 2 * pair:2 * pair + 2], z1_rstd_ready)
                for pair in (0, 1):
                    if attn:
                        pool.wait_ge(z2_var_ready, 2 * j + pair + 1)
                        inverse_root(z2_rstd[:, 2 * pair:2 * pair + 2], z2_var[:, 2 * pair:2 * pair + 2], z2_rstd_ready)

            sections(pool, emit)


_OUTS = [((128, 128, 256), 'float32')]


def kernel(**inputs):
    import numpy as _np
    import concourse.bacc as _bacc
    from concourse import mybir as _mybir
    from concourse.bass_utils import run_bass_kernel_spmd as _run

    nc = _bacc.Bacc("TRN2", target_bir_lowering=False, num_devices=1)
    p = {k.replace("L0_gnn_", "").replace("L1_gnn_", ""): _np.asarray(v) for k, v in inputs.items()}
    def columns(a):
        return a.reshape(-1, 128).T

    order = [("x", p["x"]), ("adj", p["adj"]), ("w1t", p["W1"].T), ("b1", p["b1"]), ("gamma", columns(p["gamma"])),
             ("beta", columns(p["beta"])), ("w2t", p["W2"].T), ("b2", p["b2"]), ("wqt", p["Wq"].T), ("bq", columns(p["bq"])),
             ("wkt", p["Wk"].T), ("bk", columns(p["bk"])), ("wvt", p["Wv"].T), ("bv", columns(p["bv"])), ("wot", p["Wo"].T), ("bo", p["bo"])]
    arrays, args = {}, []
    for name, a in order:
        a = _np.ascontiguousarray(a)
        arrays[f"in_{name}"] = a
        args.append(nc.dram_tensor(f"in_{name}", a.shape, _mybir.dt.from_np(a.dtype), kind="ExternalInput").ap())
    for i, (shape, dtype) in enumerate(_OUTS):
        args.append(nc.dram_tensor(f"out_{i}_dram", shape, _mybir.dt.from_np(_np.dtype(dtype)), kind="ExternalOutput").ap())
    gnn_kernel(nc, *args)
    r = _run(nc, [arrays], core_ids=[0])
    return r.results[0]["out_0_dram"]
```

```python
import concourse.bass as bass
from concourse import mybir
from contextlib import ExitStack

F32 = mybir.dt.float32
F32R = mybir.dt.float32r
BF16 = mybir.dt.bfloat16
ALU = mybir.AluOpType
ACT = mybir.ActivationFunctionType
AX = mybir.AxisListType

EPS = 1e-5
TINY = 1.1754944e-38

CONV = ["ht", "cols", "dnb", "s", "px0", "px1", "a0", "a1", "a2", "a3", "pr0", "pr1", "pr2", "pr3", "o20", "o21"]
OUT = ["ct0", "ct1", "y0", "y1"]
TILES = ["ht", "ct0", "ct1", "cols", "xt0", "xt1", "y0", "y1", "q0", "q1", "k0", "k1", "dnb", "s", "v0", "v1",
         "px0", "px1", "a0", "a1", "a2", "a3", "pt00", "pt01", "pt10", "pt11", "c0", "pr0", "pr1", "pr2", "pr3",
         "c1", "pt20", "pt21", "pt30", "pt31", "o20", "c2", "o21", "c3"]
RING = 4


class Section:

    def __init__(self, conv, attn, out, first_use, ahead=True):
        self.ahead = conv + 1 if ahead and conv is not None else None
        self.conv, self.attn, self.out, self.first_use = conv, attn, out, first_use
        self.first = isinstance(conv, int) and conv == 0
        self.tiles = [t for t in TILES if (conv if t in CONV else out if t in OUT else attn) is not None]
        self.uses = len(self.tiles) // RING

    def bank(self, tile):
        return self.tiles.index(tile) % RING

    def full(self, tile):
        return self.first_use + self.tiles.index(tile) // RING + 1

    def freed(self, tile):
        use = self.tiles.index(tile) // RING
        return None if self.first and use == 0 else self.first_use + use


def gnn_kernel(nc, x, adj, w1t, b1, gamma, beta, w2t, b2, wqt, bq, wkt, bk, wvt, bv, wot, bo, out):
    N, C, D = x.shape
    DH = w1t.shape[1]
    HEADS = 8
    HD = D // HEADS
    QSCALE = 2.0 * HD ** -0.5
    G = 4
    GROUPS = N // G
    DT, HT_ = D // C, DH // C
    QT = HEADS // DT

    ctx = ExitStack()
    with ctx:
        def sb(name, shape, dt=F32):
            return ctx.enter_context(nc.sbuf_tensor(name, shape, dt))

        def sem(name):
            return ctx.enter_context(nc.semaphore(name))

        ring = [ctx.enter_context(nc.psum_tensor(f"ring{b}", [128, 512], F32)) for b in range(RING)]
        scores = ctx.enter_context(nc.psum_tensor("scores", [128, QT, 2, DT, C], F32))

        ident_bf = sb("ident_bf", [128, 128], BF16)
        ident = sb("ident", [128, 128])
        ones_bf = sb("ones_bf", [128, 1], BF16)
        ones_r = sb("ones_r", [128, 128], F32R)
        mean_w = sb("mean_w", [128, 128])
        neg_half = sb("neg_half", [128, G])
        stage = sb("stage", [128, 2048])
        W1 = [sb(f"w1_{h}", [128, DT, DH], F32R) for h in ("hi", "lo")]
        W2 = [sb(f"w2_{h}", [128, HT_, D], F32R) for h in ("hi", "lo")]
        WQ = [sb(f"wq_{h}", [128, DT, D], F32R) for h in ("hi", "lo")]
        WK = [sb(f"wk_{h}", [128, DT, D], F32R) for h in ("hi", "lo")]
        WV = [sb(f"wv_{h}", [128, DT, D], F32R) for h in ("hi", "lo")]
        WO = [sb(f"wo_{h}", [128, DT, D], F32R) for h in ("hi", "lo")]
        b1_rows = sb("b1_rows", [128, DH], F32R)
        b1_row = sb("b1_row", [1, DH])
        bias_cols = sb("bias_cols", [128, 4, DT])
        gb_cols = sb("gb_cols", [128, 2, HT_])
        u_rows = sb("u_rows", [128, D])
        b2_rows = sb("b2_rows", [128, D])
        bo_rows = sb("bo_rows", [128, D])
        w_nat = sb("w_nat", [128, C])
        w_rest = sb("w_rest", [128, N])
        w_cols = sb("w_cols", [128, N, 4], BF16)

        x_in = sb("x_in", [128, G, D])
        adj_in = sb("adj_in", [128, G, C])
        H = sb("H", [128, G, C], BF16)
        HT = sb("HT", [128, G, C], BF16)
        wg = sb("wg", [128, G, 4], BF16)
        cd = sb("cd", [128, 2, G])
        rc = sb("rc", [128, G])
        cd_inv = sb("cd_inv", [128, 2, G])
        cd_rec = sb("cd_rec", [128, 2, G])
        cd_rest = sb("cd_rest", [128, 2, G])
        cd_part = sb("cd_part", [128, 3, 2, G], BF16)
        rs = sb("rs", [128, G])
        U = sb("U", [128, 3, G, C], BF16)
        dnb = sb("dnb", [128, G, C])
        PT = sb("PT", [128, G, C])
        PTr = sb("PTr", [128, G, C])
        px = [sb(f"px_{h}", [128, G, DT, C], F32R) for h in ("hi", "lo")]
        r = sb("r", [128, G, DH])
        r_stats = sb("r_stats", [128, G, 6])
        r_mv = sb("r_mv", [128, G, 2])
        r_var = sb("r_var", [128, G])
        r_rstd = sb("r_rstd", [128, G])
        pr = [sb(f"pr_{h}", [128, G, HT_, C], F32R) for h in ("hi", "lo")]
        res1 = sb("res1", [128, G, D])
        res1_b = sb("res1_b", [128, G, D])
        z1 = sb("z1", [128, G, D])
        z1_stats = sb("z1_stats", [128, G, 6])
        z1_mv = sb("z1_mv", [128, G, 2])
        z1_var = sb("z1_var", [128, G])
        z1_rstd = sb("z1_rstd", [128, G])
        x1 = sb("x1", [128, G, D])

        adj_mask = sb("adj_mask", [128, G, C])
        res2 = sb("res2", [128, G, D])
        xt = [sb(f"xt_{h}", [128, DT, G, C], F32R) for h in ("hi", "lo")]
        q = sb("q", [128, DT, G, C])
        k = sb("k", [128, DT, G, C])
        v = sb("v", [128, G, HEADS, HD + 1])
        sm = sb("sm", [128, G, QT, DT, C])
        mx = sb("mx", [128, G, QT, DT])
        pT = sb("pT", [128, 2, HEADS, C])
        rinv = sb("rinv", [128, G, HEADS])
        cx = sb("cx", [128, G, D])
        ct = [sb(f"ct_{h}", [128, DT, G, C], F32R) for h in ("hi", "lo")]
        z2 = sb("z2", [128, G, D])
        z2_stats = sb("z2_stats", [128, G, 6])
        z2_mv = sb("z2_mv", [128, G, 2])
        z2_var = sb("z2_var", [128, G])
        z2_rstd = sb("z2_rstd", [128, G])
        y_out = sb("y_out", [128, G, D])

        bank_full = [sem(f"bank_full{b}") for b in range(RING)]
        bank_free = [sem(f"bank_free{b}") for b in range(RING)]
        scores_full, scores_free = sem("scores_full"), sem("scores_free")
        const_ready, weights_in, weights_ready = sem("const_ready"), sem("weights_in"), sem("weights_ready")
        prep_dve, prep_pe, b1_step = sem("prep_dve"), sem("prep_pe"), sem("b1_step")
        prep_step = sem("prep_step")
        x_loaded, adj_loaded, mask_loaded, stored = sem("x_loaded"), sem("adj_loaded"), sem("mask_loaded"), sem("stored")
        h_ready, ht_ready, wg_ready = sem("h_ready"), sem("ht_ready"), sem("wg_ready")
        cols_step, u_ready, dnb_ready, pt_ready, ptr_ready = (
            sem("cols_step"), sem("u_ready"), sem("dnb_ready"), sem("pt_ready"), sem("ptr_ready"))
        px_hi, px_lo, r_ready, pr_hi, pr_lo = sem("px_hi"), sem("px_lo"), sem("r_ready"), sem("pr_hi"), sem("pr_lo")
        r_read = sem("r_read")
        r_step, r_var_ready, r_rstd_ready = sem("r_step"), sem("r_var_ready"), sem("r_rstd_ready")
        res1_step, z1_step, z1_var_ready, z1_rstd_ready, x1_ready = (
            sem("res1_step"), sem("z1_step"), sem("z1_var_ready"), sem("z1_rstd_ready"), sem("x1_ready"))
        res2_ready, xt_hi, xt_lo = sem("res2_ready"), sem("xt_hi"), sem("xt_lo")
        qk_ready, v_ready = sem("qk_ready"), sem("v_ready")
        sm_ready, mx_ready, sub_ready, p_ready = sem("sm_ready"), sem("mx_ready"), sem("sub_ready"), sem("p_ready")
        rinv_ready, cx_ready, ct_hi, ct_lo = sem("rinv_ready"), sem("cx_ready"), sem("ct_hi"), sem("ct_lo")
        z2_step, z2_var_ready, z2_rstd_ready, y_ready = (
            sem("z2_step"), sem("z2_var_ready"), sem("z2_rstd_ready"), sem("y_ready"))

        x_g = x.rearrange("n c d -> c n d")
        adj_g = adj.rearrange("n c e -> c n e")
        out_g = out.rearrange("n c d -> c n d")
        WEIGHT_LOADS = 15
        Z2_STEPS = 2 + 2 * G
        COLS_STEPS = 12

        def sections(eng, emit):
            uses = len(TILES) // RING
            s = Section(0, None, None, 0)
            emit(s)
            at = s.uses
            s = Section(1, 0, None, at)
            emit(s)
            at += s.uses
            with eng.Fori(1, GROUPS - 2) as j:
                emit(Section(j + 1, j, j - 1, (j - 1) * uses + at))
            at += (GROUPS - 3) * uses
            s = Section(GROUPS - 1, GROUPS - 2, GROUPS - 3, at, ahead=False)
            emit(s)
            at += s.uses
            s = Section(None, GROUPS - 1, GROUPS - 2, at)
            emit(s)
            emit(Section(None, None, GROUPS - 1, at + s.uses))

        block = ctx.enter_context(nc.Block())

        @block.sync
        def _(sp):
            def load(dst, src):
                sp.dma_start(dst, src).then_inc(weights_in, 16)

            sp.dma_start(w_nat[0:N, :], adj[:, 0, :]).then_inc(weights_in, 16)
            sp.dma_start(adj_in[:], adj_g[:, 0:G, :]).then_inc(adj_loaded, 16)
            sp.dma_start(x_in[:], x_g[:, 0:G, :]).then_inc(x_loaded, 16)
            for wt, place in ((w1t, 0), (w2t, 1024)):
                load(stage[:, place:place + 1024].rearrange("p (t n) -> p t n", t=wt.shape[0] // 128),
                     wt.rearrange("(t p) n -> p t n", p=128))
            load(b1_row[:], b1.rearrange("(a n) -> a n", a=1))
            for n, b in enumerate((bq, bk, bv)):
                load(bias_cols[:, n, :], b)
            for n, b in enumerate((gamma, beta)):
                load(gb_cols[:, n, :], b)
            for rows, b in ((b2_rows, b2), (bo_rows, bo)):
                load(rows[:], b.rearrange("(a n) -> a n", a=1).partition_broadcast(128))
            for n, wt in enumerate((wqt, wkt, wvt, wot)):
                load((res2, z2, cx, y_out)[n][:, 0:2, :], wt.rearrange("(t p) n -> p t n", p=128))

            sp.dma_start(adj_mask[:], adj_g[:, 0:G, :]).then_inc(mask_loaded, 16)
            def emit(s):
                i, j, o = s.conv, s.attn, s.out
                if s.ahead is not None:
                    sp.wait_ge(h_ready, i + 1)
                    sp.dma_start(adj_in[:], adj_g[:, bass.ds(i * G + G, G), :]).then_inc(adj_loaded, 16)
                    sp.wait_ge(px_hi, 2 * i + 2)
                    sp.wait_ge(res1_step, 3 * i + 3)
                    sp.dma_start(x_in[:], x_g[:, bass.ds(i * G + G, G), :]).then_inc(x_loaded, 16)
                if o is not None:
                    sp.wait_ge(y_ready, G * o + G)
                    sp.dma_start(out_g[:, bass.ds(o * G, G), :], y_out[:]).then_inc(stored, 16)
                if j is not None and i is not None:
                    sp.wait_ge(sm_ready, G * j + G)
                    sp.dma_start(adj_mask[:], adj_g[:, bass.ds(j * G + G, G), :]).then_inc(mask_loaded, 16)

            sections(sp, emit)
            sp.wait_ge(stored, 16 * GROUPS + 16)

        @block.tensor
        def _(pe):
            mm = nc.tensor.matmul

            def claim(s, tile):
                if s.freed(tile) is not None:
                    pe.wait_ge(bank_free[s.bank(tile)], s.freed(tile))
                return ring[s.bank(tile)]

            def split_product(dst, lhs, rhs, extra=None):
                (a_hi, a_lo), (b_hi, b_lo) = lhs, rhs
                n = len(a_hi)
                pairs = [(a_hi[t], b_hi[t]) for t in range(n)] + [(a_hi[t], b_lo[t]) for t in range(n)]
                pairs += [(a_lo[t], b_hi[t]) for t in range(n)]
                if extra:
                    pairs = [extra] + pairs
                for m, (a, b) in enumerate(pairs):
                    last = mm(dst, a, b, start=(m == 0), stop=(m == len(pairs) - 1))
                return last

            pe.wait_ge(const_ready, 8)
            pe.wait_ge(prep_dve, 5)
            w2g = sm[:, 0, 0:QT, :, :].rearrange("p a b c -> p (a b c)")
            nc.tensor.transpose(ring[0][:, 0:N], w_nat[0:N, :], ident[0:N, 0:N]).then_inc(prep_pe, 1)
            for t in range(HT_):
                last = mm(ring[1][:, 0:D], mean_w[:], w2g[:, t * D:(t + 1) * D], start=t == 0, stop=t == HT_ - 1)
            last.then_inc(prep_pe, 1)
            for t in range(HT_):
                last = mm(ring[2][:, 0:D], gb_cols[:, 1, t:t + 1].broadcast_to([128, 128]),
                          stage[:, 1024 + t * D:1024 + (t + 1) * D], start=t == 0, stop=t == HT_ - 1)
            last.then_inc(prep_pe, 1)
            for t in range(DT):
                last = mm(ring[3][:, 0:D], bias_cols[:, 2, t:t + 1].broadcast_to([128, 128]), y_out[:, t, :],
                          start=t == 0, stop=t == DT - 1)
            last.then_inc(prep_pe, 1)
            pe.wait_ge(weights_ready, 1)

            def incidence_transposed(s, i):
                bank = claim(s, "ht")
                pe.wait_ge(h_ready, i + 1)
                dst = bank[:, 0:G * C // 2].bitcast(BF16)
                for g in range(G):
                    last = nc.tensor.transpose(dst[:, g * C:(g + 1) * C], H[:, g, :], ident_bf[:])
                last.then_inc(bank_full[s.bank("ht")], 1)

            def degree_columns(s, i):
                bank = claim(s, "cols")
                pe.wait_ge(ht_ready, i + 1)
                pe.wait_ge(wg_ready, i + 1)
                for g in range(G):
                    mm(bank[:, 8 * g:8 * g + 4], HT[:, g, :], wg[:, g, :], start=True, stop=True)
                    last = mm(bank[:, 8 * g + 4:8 * g + 5], H[:, g, :], ones_bf[:], start=True, stop=True)
                last.then_inc(bank_full[s.bank("cols")], 1)

            def degree_rows(s, i):
                bank = claim(s, "dnb")
                pe.wait_ge(cols_step, COLS_STEPS * i + COLS_STEPS)
                for g in range(G):
                    for m in range(3):
                        last = mm(bank[:, g * C:(g + 1) * C], cd_part[:, m, 1, g:g + 1].broadcast_to([128, 128]),
                                  ident_bf[:], start=m == 0, stop=m == 2)
                last.then_inc(bank_full[s.bank("dnb")], 1)

            def shared_edges(s, i):
                bank = claim(s, "s")
                pe.wait_ge(u_ready, 3 * i + 3)
                for g in range(G):
                    for m in range(3):
                        last = mm(bank[:, g * C:(g + 1) * C], HT[:, g, :], U[:, m, g, :], start=m == 0, stop=m == 2)
                last.then_inc(bank_full[s.bank("s")], 1)

            def propagate_x(s, i, pair):
                tile = f"px{pair}"
                bank = claim(s, tile)
                if pair == 0:
                    pe.wait_ge(pt_ready, i + 1)
                    pe.wait_ge(x_loaded, 16 * i + 16)
                for g in (0, 1):
                    for t in range(DT):
                        at = (g * DT + t) * C
                        last = mm(bank[:, at:at + C], x_in[:, 2 * pair + g, t * C:(t + 1) * C], PT[:, 2 * pair + g, :],
                                  start=True, stop=True)
                last.then_inc(bank_full[s.bank(tile)], 1)

            def hidden(s, i, g):
                tile = f"a{g}"
                bank = claim(s, tile)
                pe.wait_ge(px_lo, 2 * i + g // 2 + 1)
                split_product(bank[:], [[p[:, g, t, :] for t in range(DT)] for p in px],
                              [[w[:, t, :] for t in range(DT)] for w in W1],
                              extra=(ones_r[:], b1_rows[:])).then_inc(bank_full[s.bank(tile)], 1)

            def propagate_r(s, i, g):
                tile = f"pr{g}"
                bank = claim(s, tile)
                if g == 0:
                    pe.wait_ge(ptr_ready, i + 1)
                for t in range(HT_):
                    last = mm(bank[:, t * C:(t + 1) * C], r[:, g, t * C:(t + 1) * C], PTr[:, g, :], start=True, stop=True)
                last.then_inc(bank_full[s.bank(tile)], 1)

            def second_conv(s, i, pair):
                tile = f"o2{pair}"
                bank = claim(s, tile)
                for g in (0, 1):
                    pe.wait_ge(pr_lo, G * i + 2 * pair + g + 1)
                    last = split_product(bank[:, g * D:(g + 1) * D],
                                         [[p[:, 2 * pair + g, t, :] for t in range(HT_)] for p in pr],
                                         [[w[:, t, :] for t in range(HT_)] for w in W2])
                last.then_inc(bank_full[s.bank(tile)], 1)

            def x1_transposed(s, j, t):
                tile = f"xt{t}"
                bank = claim(s, tile)
                if t == 0:
                    pe.wait_ge(x1_ready, G * j + G)
                for g in range(G):
                    last = nc.tensor.transpose(bank[:, g * C:(g + 1) * C], x1[:, g, t * C:(t + 1) * C], ident[:])
                last.then_inc(bank_full[s.bank(tile)], 1)

            def queries_keys(s, j, name, weights, f):
                tile = f"{name}{f}"
                bank = claim(s, tile)
                pe.wait_ge(xt_lo, 2 * j + 2)
                split_product(bank[:], [[w[:, t, f * C:(f + 1) * C] for t in range(DT)] for w in weights],
                              [[a[:, t, :, :].rearrange("p g c -> p (g c)") for t in range(DT)] for a in xt]
                              ).then_inc(bank_full[s.bank(tile)], 1)

            def values(s, j, pair):
                tile = f"v{pair}"
                bank = claim(s, tile)
                for g in (0, 1):
                    last = split_product(bank[:, g * D:(g + 1) * D],
                                         [[a[:, t, 2 * pair + g, :] for t in range(DT)] for a in xt],
                                         [[w[:, t, :] for t in range(DT)] for w in WV])
                last.then_inc(bank_full[s.bank(tile)], 1)

            def score_pair(s, j, pair):
                if pair == 0:
                    pe.wait_ge(qk_ready, 4 * j + 4)
                pe.wait_ge(scores_free, 2 * j + pair + 1)
                for g in (0, 1):
                    for t in range(DT):
                        for h in range(QT):
                            rows = slice(h * HD, (h + 1) * HD)
                            last = mm(scores[:, h, g, t, :], q[rows, t, 2 * pair + g, :], k[rows, t, 2 * pair + g, :],
                                      start=True, stop=True)
                last.then_inc(scores_full, 1)

            def scores_transposed(s, j, g, t):
                tile = f"pt{g}{t}"
                bank = claim(s, tile)
                pe.wait_ge(sub_ready, G * j + g + 1)
                for h in range(QT):
                    last = nc.tensor.transpose(bank[:, h * C:(h + 1) * C], sm[:, g, h, t, :], ident[:])
                last.then_inc(bank_full[s.bank(tile)], 1)

            def context(s, j, g):
                tile = f"c{g}"
                bank = claim(s, tile)
                pe.wait_ge(p_ready, DT * (G * j + g + 1))
                if g == 0:
                    pe.wait_ge(v_ready, 2 * j + 2)
                for h in range(HEADS):
                    last = mm(bank[:, h * (HD + 1):(h + 1) * (HD + 1)], pT[:, g % 2, h, :], v[:, g, h, :],
                              start=True, stop=True)
                last.then_inc(bank_full[s.bank(tile)], 1)

            def context_transposed(s, j, t):
                tile = f"ct{t}"
                bank = claim(s, tile)
                if t == 0:
                    pe.wait_ge(cx_ready, G * j + G)
                for g in range(G):
                    last = nc.tensor.transpose(bank[:, g * C:(g + 1) * C], cx[:, g, t * C:(t + 1) * C], ident[:])
                last.then_inc(bank_full[s.bank(tile)], 1)

            def output(s, j, pair):
                tile = f"y{pair}"
                bank = claim(s, tile)
                if pair == 0:
                    pe.wait_ge(ct_lo, 2 * j + 2)
                for g in (0, 1):
                    last = split_product(bank[:, g * D:(g + 1) * D],
                                         [[a[:, t, 2 * pair + g, :] for t in range(DT)] for a in ct],
                                         [[w[:, t, :] for t in range(DT)] for w in WO])
                last.then_inc(bank_full[s.bank(tile)], 1)

            def emit(s):
                i, j, o = s.conv, s.attn, s.out
                conv, attn, out_ = i is not None, j is not None, o is not None
                if conv:
                    incidence_transposed(s, i)
                if out_:
                    context_transposed(s, o, 0)
                    context_transposed(s, o, 1)
                if conv:
                    degree_columns(s, i)
                if attn:
                    x1_transposed(s, j, 0)
                    x1_transposed(s, j, 1)
                if out_:
                    output(s, o, 0)
                    output(s, o, 1)
                if attn:
                    queries_keys(s, j, "q", WQ, 0)
                    queries_keys(s, j, "q", WQ, 1)
                    queries_keys(s, j, "k", WK, 0)
                    queries_keys(s, j, "k", WK, 1)
                if conv:
                    degree_rows(s, i)
                    shared_edges(s, i)
                if attn:
                    values(s, j, 0)
                    values(s, j, 1)
                if conv:
                    propagate_x(s, i, 0)
                    propagate_x(s, i, 1)
                if attn:
                    score_pair(s, j, 0)
                if conv:
                    hidden(s, i, 0)
                    hidden(s, i, 1)
                if attn:
                    score_pair(s, j, 1)
                if conv:
                    hidden(s, i, 2)
                    hidden(s, i, 3)
                if attn:
                    for g in (0, 1):
                        scores_transposed(s, j, g, 0)
                        scores_transposed(s, j, g, 1)
                    context(s, j, 0)
                if conv:
                    for g in range(G):
                        propagate_r(s, i, g)
                if attn:
                    context(s, j, 1)
                    for g in (2, 3):
                        scores_transposed(s, j, g, 0)
                        scores_transposed(s, j, g, 1)
                if conv:
                    second_conv(s, i, 0)
                if attn:
                    context(s, j, 2)
                if conv:
                    second_conv(s, i, 1)
                if attn:
                    context(s, j, 3)

            sections(pe, emit)

        @block.scalar
        def _(act):
            def filled(s, tile):
                act.wait_ge(bank_full[s.bank(tile)], s.full(tile))
                return ring[s.bank(tile)]

            act.wait_ge(weights_ready, 1)

            def copy(dst, src):
                return nc.scalar.activation(dst, src, ACT.Copy)

            def incidence_transposed(s, i):
                bank = filled(s, "ht")
                copy(HT[:].rearrange("p g c -> p (g c)"), bank[:, 0:G * C // 2].bitcast(BF16)).then_inc(ht_ready, 1)
                act.wait_ge(ht_ready, i + 1)
                act.sem_inc(bank_free[s.bank("ht")], 1)

            def degree_rows(s, i):
                bank = filled(s, "dnb")
                copy(dnb[:].rearrange("p g c -> p (g c)"), bank[:]).then_inc(dnb_ready, 1)
                act.wait_ge(dnb_ready, i + 1)
                act.sem_inc(bank_free[s.bank("dnb")], 1)

            def px_high(s, i, pair):
                bank = filled(s, f"px{pair}")
                copy(px[0][:, 2 * pair:2 * pair + 2, :, :].rearrange("p g t c -> p (g t c)"), bank[:]).then_inc(px_hi, 1)

            def relu(s, i, g):
                bank = filled(s, f"a{g}")
                if g == 0 and not s.first:
                    act.wait_ge(r_read, G * i)
                nc.scalar.activation(r[:, g, :], bank[:], ACT.Relu).then_inc(r_ready, 1)
                act.wait_ge(r_ready, G * i + g + 1)
                act.sem_inc(bank_free[s.bank(f"a{g}")], 1)

            def pr_high(s, i, g):
                bank = filled(s, f"pr{g}")
                copy(pr[0][:, g, :, :].rearrange("p t c -> p (t c)"), bank[:]).then_inc(pr_hi, 1)

            def xt_high(s, j, t):
                bank = filled(s, f"xt{t}")
                copy(xt[0][:, t, :, :].rearrange("p g c -> p (g c)"), bank[:]).then_inc(xt_hi, 1)

            def queries_keys(s, j, name, dst, bias, f, n):
                bank = filled(s, f"{name}{f}")
                nc.scalar.activation(dst[:, f, :, :].rearrange("p g c -> p (g c)"), bank[:], ACT.Identity,
                                     bias=bias_cols[:, bias, f:f + 1]).then_inc(qk_ready, 1)
                act.wait_ge(qk_ready, 4 * j + n)
                act.sem_inc(bank_free[s.bank(f"{name}{f}")], 1)

            def values(s, j, pair):
                bank = filled(s, f"v{pair}")
                copy(v[:, 2 * pair:2 * pair + 2, :, 0:HD],
                     bank[:].rearrange("p (g h d) -> p g h d", g=2, h=HEADS)).then_inc(v_ready, 1)
                act.wait_ge(v_ready, 2 * j + pair + 1)
                act.sem_inc(bank_free[s.bank(f"v{pair}")], 1)

            def exponential(s, j, g, t):
                bank = filled(s, f"pt{g}{t}")
                nc.scalar.activation(pT[:, g % 2, t * QT:(t + 1) * QT, :].rearrange("p h c -> p (h c)"), bank[:],
                                     ACT.Exp).then_inc(p_ready, 1)
                act.wait_ge(p_ready, DT * (G * j + g) + t + 1)
                act.sem_inc(bank_free[s.bank(f"pt{g}{t}")], 1)

            def ct_high(s, j, t):
                bank = filled(s, f"ct{t}")
                copy(ct[0][:, t, :, :].rearrange("p g c -> p (g c)"), bank[:]).then_inc(ct_hi, 1)

            def emit(s):
                i, j, o = s.conv, s.attn, s.out
                conv, attn, out_ = i is not None, j is not None, o is not None
                if conv:
                    incidence_transposed(s, i)
                if out_:
                    ct_high(s, o, 0)
                    ct_high(s, o, 1)
                if attn:
                    xt_high(s, j, 0)
                    xt_high(s, j, 1)
                    queries_keys(s, j, "q", q, 0, 0, 1)
                    queries_keys(s, j, "q", q, 0, 1, 2)
                    queries_keys(s, j, "k", k, 1, 0, 3)
                    queries_keys(s, j, "k", k, 1, 1, 4)
                if conv:
                    degree_rows(s, i)
                if attn:
                    values(s, j, 0)
                    values(s, j, 1)
                if conv:
                    px_high(s, i, 0)
                    px_high(s, i, 1)
                    for g in range(G):
                        relu(s, i, g)
                if attn:
                    for g in (0, 1):
                        exponential(s, j, g, 0)
                        exponential(s, j, g, 1)
                if conv:
                    for g in range(G):
                        pr_high(s, i, g)
                if attn:
                    act.wait_ge(bank_full[s.bank("c1")], s.full("c1"))
                    for g in (2, 3):
                        exponential(s, j, g, 0)
                        exponential(s, j, g, 1)

            sections(act, emit)



        @block.vector
        def _(dve):
            V = nc.vector

            def filled(s, tile):
                dve.wait_ge(bank_full[s.bank(tile)], s.full(tile))
                return ring[s.bank(tile)]

            V.memset(b1_rows[:].bitcast(F32), 0.0).then_inc(prep_dve, 1)
            dve.wait_ge(weights_in, 16 * WEIGHT_LOADS)
            dve.wait_ge(prep_dve, 1)
            V.tensor_copy(b1_rows[0:1, :], b1_row[:]).then_inc(b1_step, 1)
            dve.wait_ge(b1_step, 1)
            V.tensor_tensor(b1_rows[32:33, :], b1_row[:], b1_rows[0:1, :].bitcast(F32), ALU.subtract).then_inc(prep_dve, 1)
            count = [0]

            def step(ins):
                count[0] += 1
                ins.then_inc(prep_step, 1)
                dve.wait_ge(prep_step, count[0])

            def split(hi, lo, src):
                step(V.tensor_copy(hi, src))
                step(V.tensor_tensor(lo, src, hi.bitcast(F32), ALU.subtract))

            w2_in = stage[:, 1024:2048].rearrange("p (t n) -> p t n", t=HT_)
            w2g = sm[:, 0, 0:QT, :, :].rearrange("p a b c -> p (a b c)").rearrange("p (t n) -> p t n", t=HT_)
            for t in range(HT_):
                step(V.tensor_scalar(w2g[:, t, :], w2_in[:, t, :], gb_cols[:, 0, t:t + 1], None, ALU.mult))
            step(V.memset(w_cols[:], 1.0))
            step(V.memset(v[:], 1.0))
            dve.sem_inc(prep_dve, 3)
            step(V.tensor_scalar(res2[:, 0:2, :], res2[:, 0:2, :], QSCALE, None, ALU.mult))
            step(V.tensor_scalar(bias_cols[:, 0, :], bias_cols[:, 0, :], QSCALE, None, ALU.mult))
            split(W1[0][:].rearrange("p t n -> p (t n)"), W1[1][:].rearrange("p t n -> p (t n)"), stage[:, 0:1024])
            for w, src in ((WQ, res2), (WK, z2), (WV, cx), (WO, y_out)):
                split(w[0][:], w[1][:], src[:, 0:2, :])
            dve.wait_ge(prep_pe, 1)
            step(V.tensor_copy(w_cols[:, :, 0], ring[0][:, 0:N]))
            step(V.tensor_tensor(w_rest[:], ring[0][:, 0:N], w_cols[:, :, 0], ALU.subtract))
            step(V.tensor_copy(w_cols[:, :, 1], w_rest[:]))
            step(V.tensor_tensor(w_cols[:, :, 2], w_rest[:], w_cols[:, :, 1], ALU.subtract))
            dve.wait_ge(prep_pe, 2)
            for t in range(HT_):
                step(V.tensor_tensor(w2g[:, t, :], w2g[:, t, :], ring[1][:, 0:D], ALU.subtract))
            split(W2[0][:], W2[1][:], w2g)
            dve.wait_ge(prep_pe, 3)
            step(V.tensor_copy(u_rows[:], ring[2][:, 0:D]))
            dve.wait_ge(prep_pe, 4)
            step(V.tensor_tensor(bo_rows[:], bo_rows[:], ring[3][:, 0:D], ALU.add))
            dve.sem_inc(weights_ready, 1)

            def incidence(i):
                dve.wait_ge(adj_loaded, 16 * i + 16)
                V.tensor_scalar(H[:], adj_in[:], 0.0, None, ALU.not_equal).then_inc(h_ready, 1)
                V.tensor_copy(wg[:], w_cols[:, bass.ds(i * G, G), :]).then_inc(wg_ready, 1)

            def degrees(s, i):
                bank = filled(s, "cols")
                cols = bank[:, 0:8 * G].rearrange("p (g m) -> p g m", m=8)
                n = [0]

                def link(ins):
                    n[0] += 1
                    ins.then_inc(cols_step, 1)
                    dve.wait_ge(cols_step, COLS_STEPS * i + n[0])

                V.tensor_copy(cd[:, 0, :], cols[:, :, 4]).then_inc(cols_step, 1)
                V.tensor_copy(rc[:], cols[:, :, 3]).then_inc(cols_step, 1)
                n[0] = 2
                link(V.tensor_reduce(cd[:, 1, :], cols[:, :, 0:3], AX.X, ALU.add))
                dve.sem_inc(bank_free[s.bank("cols")], 1)
                link(V.tensor_scalar(cd_inv[:], cd[:], TINY, None, ALU.max))
                link(V.reciprocal(cd_rest[:], cd_inv[:]))
                link(V.scalar_tensor_tensor(out=cd_rec[:], in0=cd[:], scalar=0.0, in1=cd_rest[:],
                                            op0=ALU.is_gt, op1=ALU.mult))
                link(V.tensor_copy(cd_part[:, 0, :, :], cd_rec[:]))
                link(V.tensor_tensor(cd_inv[:], cd_rec[:], cd_part[:, 0, :, :], ALU.subtract))
                link(V.tensor_copy(cd_part[:, 1, :, :], cd_inv[:]))
                link(V.tensor_tensor(cd_rest[:], cd_inv[:], cd_part[:, 1, :, :], ALU.subtract))
                link(V.tensor_copy(cd_part[:, 2, :, :], cd_rest[:]))
                link(V.tensor_tensor(rs[:], cd_rec[:, 1, :], rc[:], ALU.mult))
                assert n[0] == COLS_STEPS

            def edge_weights(s, i):
                for m in range(3):
                    V.tensor_tensor(U[:, m, :, :], HT[:],
                                    cd_part[:, m, 0, :].unsqueeze(2).broadcast_to([128, G, C]), ALU.mult).then_inc(u_ready, 1)

            def propagator(s, i):
                bank = filled(s, "s")
                dve.wait_ge(dnb_ready, i + 1)
                V.tensor_tensor(PT[:].rearrange("p g c -> p (g c)"), bank[:],
                                dnb[:].rearrange("p g c -> p (g c)"), ALU.mult).then_inc(pt_ready, 1)
                dve.wait_ge(pt_ready, i + 1)
                dve.sem_inc(bank_free[s.bank("s")], 1)

            def low_half(s, tile, halves, hi_sem, lo_sem, value):
                bank = ring[s.bank(tile)]
                dve.wait_ge(hi_sem, value)
                V.tensor_tensor(halves[1], bank[:], halves[0].bitcast(F32), ALU.subtract).then_inc(lo_sem, 1)
                dve.wait_ge(lo_sem, value)
                dve.sem_inc(bank_free[s.bank(tile)], 1)

            def px_low(s, i, pair):
                low_half(s, f"px{pair}", [p[:, 2 * pair:2 * pair + 2, :, :].rearrange("p g t c -> p (g t c)") for p in px],
                         px_hi, px_lo, 2 * i + pair + 1)

            def hidden_stats(s, i, g):
                dve.wait_ge(r_ready, G * i + g + 1)
                V.bn_stats(r_stats[:, g, :], r[:, g, :]).then_inc(r_step, 1)
                dve.wait_ge(r_step, 2 * G * i + 2 * g + 1)
                dve.sem_inc(r_read, 1)
                V.bn_aggr(r_mv[:, g, :], r_stats[:, g, :]).then_inc(r_step, 1)

            def hidden_scale(s, i):
                dve.wait_ge(r_step, 2 * G * i + 2 * G)
                V.tensor_scalar(r_var[:], r_mv[:, :, 1], EPS, None, ALU.add).then_inc(r_var_ready, 1)

            def scaled_propagator(s, i):
                dve.wait_ge(r_rstd_ready, i + 1)
                V.tensor_tensor(PTr[:], PT[:], r_rstd[:].unsqueeze(2).broadcast_to([128, G, C]),
                                ALU.mult).then_inc(ptr_ready, 1)

            def pr_low(s, i, g):
                low_half(s, f"pr{g}", [p[:, g, :, :].rearrange("p t c -> p (t c)") for p in pr], pr_hi, pr_lo, G * i + g + 1)

            def residual_stats(s, i, pair):
                bank = filled(s, f"o2{pair}")
                if pair == 0:
                    dve.wait_ge(res1_step, 3 * i + 3)
                two = slice(2 * pair, 2 * pair + 2)
                base = 10 * i + 5 * pair
                V.tensor_tensor(z1[:, two, :].rearrange("p g d -> p (g d)"), bank[:],
                                res1[:, two, :].rearrange("p g d -> p (g d)"), ALU.add).then_inc(z1_step, 1)
                dve.wait_ge(z1_step, base + 1)
                for g in (2 * pair, 2 * pair + 1):
                    V.bn_stats(z1_stats[:, g, :], z1[:, g, :]).then_inc(z1_step, 1)
                dve.wait_ge(z1_step, base + 3)
                dve.sem_inc(bank_free[s.bank(f"o2{pair}")], 1)
                for g in (2 * pair, 2 * pair + 1):
                    V.bn_aggr(z1_mv[:, g, :], z1_stats[:, g, :]).then_inc(z1_step, 1)
                dve.wait_ge(z1_step, base + 5)
                V.tensor_scalar(z1_var[:, two], z1_mv[:, two, 1], EPS, None, ALU.add).then_inc(z1_var_ready, 1)

            def output_residual(s, o):
                dve.wait_ge(res2_ready, o + 1)
                for pair in (0, 1):
                    two = slice(2 * pair, 2 * pair + 2)
                    bank = filled(s, f"y{pair}")
                    V.tensor_tensor(z2[:, two, :].rearrange("p g d -> p (g d)"), bank[:],
                                    res2[:, two, :].rearrange("p g d -> p (g d)"), ALU.add).then_inc(z2_step, 1)
                dve.wait_ge(z2_step, Z2_STEPS * o + 2)
                dve.sem_inc(bank_free[s.bank("y0")], 1)
                dve.sem_inc(bank_free[s.bank("y1")], 1)

            def output_stats(s, o):
                for g in range(G):
                    V.bn_stats(z2_stats[:, g, :], z2[:, g, :]).then_inc(z2_step, 1)
                dve.wait_ge(z2_step, Z2_STEPS * o + 2 + G)

            def output_variance(s, o):
                for g in range(G):
                    V.bn_aggr(z2_mv[:, g, :], z2_stats[:, g, :]).then_inc(z2_step, 1)
                dve.wait_ge(z2_step, Z2_STEPS * o + 2 + 2 * G)
                V.tensor_scalar(z2_var[:], z2_mv[:, :, 1], EPS, None, ALU.add).then_inc(z2_var_ready, 1)

            def normalise(ready, graphs, rstd_value, dst, z, mv, rstd, rstd_ready):
                dve.wait_ge(rstd_ready, rstd_value)
                for g in graphs:
                    V.tensor_scalar(dst[:, g, :], z[:, g, :], mv[:, g, 0:1], rstd[:, g:g + 1],
                                    ALU.subtract, ALU.mult).then_inc(ready, 1)

            def xt_low(s, j, t):
                low_half(s, f"xt{t}", [a[:, t, :, :].rearrange("p g c -> p (g c)") for a in xt], xt_hi, xt_lo, 2 * j + t + 1)

            def mask_scores(s, j, pair):
                dve.wait_ge(scores_full, 2 * j + pair + 1)
                if pair == 0:
                    dve.wait_ge(mask_loaded, 16 * j + 16)
                for g in (0, 1):
                    V.tensor_tensor(sm[:, 2 * pair + g, :, :, :], scores[:, :, g, :, :],
                                    adj_mask[:, 2 * pair + g, :].unsqueeze(1).unsqueeze(1).broadcast_to([128, QT, DT, C]),
                                    ALU.mult).then_inc(sm_ready, 1)
                dve.wait_ge(sm_ready, G * j + 2 * pair + 2)
                dve.sem_inc(scores_free, 1)

            def row_max(s, j, g):
                V.tensor_reduce(mx[:, g, :, :], sm[:, g, :, :, :], AX.X, ALU.max).then_inc(mx_ready, 1)

            def context(s, j, g):
                bank = filled(s, f"c{g}")
                heads = bank[:, 0:HEADS * (HD + 1)].rearrange("p (h d) -> p h d", h=HEADS)
                V.reciprocal(rinv[:, g, :], heads[:, :, HD]).then_inc(rinv_ready, 1)
                dve.wait_ge(rinv_ready, G * j + g + 1)
                V.tensor_tensor(cx[:, g, :].rearrange("p (h d) -> p h d", h=HEADS), heads[:, :, 0:HD],
                                rinv[:, g, :].unsqueeze(2).broadcast_to([128, HEADS, HD]), ALU.mult).then_inc(cx_ready, 1)
                dve.wait_ge(cx_ready, G * j + g + 1)
                dve.sem_inc(bank_free[s.bank(f"c{g}")], 1)

            def ct_low(s, j, t):
                low_half(s, f"ct{t}", [a[:, t, :, :].rearrange("p g c -> p (g c)") for a in ct], ct_hi, ct_lo, 2 * j + t + 1)

            def emit(s):
                i, j, o = s.conv, s.attn, s.out
                conv, attn, out_ = i is not None, j is not None, o is not None
                if s.first:
                    incidence(0)
                if out_:
                    ct_low(s, o, 0)
                    ct_low(s, o, 1)
                if attn:
                    xt_low(s, j, 0)
                    xt_low(s, j, 1)
                if conv:
                    degrees(s, i)
                if out_:
                    output_residual(s, o)
                if conv:
                    edge_weights(s, i)
                if out_:
                    output_stats(s, o)
                if conv:
                    propagator(s, i)
                    px_low(s, i, 0)
                if out_:
                    output_variance(s, o)
                if conv:
                    px_low(s, i, 1)
                if s.ahead is not None:
                    incidence(s.ahead)
                if out_:
                    dve.wait_ge(stored, 16 * o + 16)
                    normalise(y_ready, range(G), o + 1, y_out, z2, z2_mv, z2_rstd, z2_rstd_ready)
                if attn:
                    mask_scores(s, j, 0)
                if attn:
                    row_max(s, j, 0)
                    row_max(s, j, 1)
                if conv:
                    hidden_stats(s, i, 0)
                    hidden_stats(s, i, 1)
                if attn:
                    mask_scores(s, j, 1)
                if conv:
                    hidden_stats(s, i, 2)
                    hidden_stats(s, i, 3)
                    hidden_scale(s, i)
                if attn:
                    row_max(s, j, 2)
                if conv:
                    scaled_propagator(s, i)
                if attn:
                    row_max(s, j, 3)
                    context(s, j, 0)
                if conv:
                    for g in range(G):
                        pr_low(s, i, g)
                if attn:
                    context(s, j, 1)
                if conv:
                    residual_stats(s, i, 0)
                if attn:
                    context(s, j, 2)
                if conv:
                    normalise(x1_ready, range(2), 2 * i + 1, x1, z1, z1_mv, z1_rstd, z1_rstd_ready)
                    residual_stats(s, i, 1)
                if attn:
                    context(s, j, 3)
                if conv:
                    normalise(x1_ready, range(2, 4), 2 * i + 2, x1, z1, z1_mv, z1_rstd, z1_rstd_ready)

            sections(dve, emit)

        @block.gpsimd
        def _(pool):
            P = nc.gpsimd
            P.memset(ident_bf[:], 0.0).then_inc(const_ready, 1)
            P.memset(ident[:], 0.0).then_inc(const_ready, 1)
            P.memset(ones_bf[:], 1.0).then_inc(const_ready, 1)
            P.memset(ones_r[:].bitcast(F32), 1.0).then_inc(const_ready, 1)
            P.memset(mean_w[:], 1.0 / DH).then_inc(const_ready, 1)
            P.memset(neg_half[:], -0.5).then_inc(const_ready, 1)
            pool.wait_ge(const_ready, 6)
            for m in (ident_bf, ident):
                P.affine_select(out=m[:], in_=m[:], compare_op=ALU.not_equal, fill=1.0, base=0,
                                pattern=[[-1, 128]], channel_multiplier=1).then_inc(const_ready, 1)
            pool.sem_inc(scores_free, 1)
            pool.sem_inc(stored, 16)
            pool.wait_ge(weights_ready, 1)

            def inverse_root(rstd, var, ready):
                P.tensor_tensor(rstd, var, neg_half[:, 0:var.shape[1]], ALU.pow).then_inc(ready, 1)

            def residual1(s, i):
                pool.wait_ge(x_loaded, 16 * i + 16)
                P.tensor_tensor(res1_b[:], x_in[:], x_in[:], ALU.add).then_inc(res1_step, 1)
                pool.wait_ge(cols_step, COLS_STEPS * i + COLS_STEPS)
                pool.wait_ge(res1_step, 3 * i + 1)
                P.tensor_tensor(res1_b[:], res1_b[:], b2_rows[:].unsqueeze(1).broadcast_to([128, G, D]), ALU.add)
                for g in range(G):
                    last = P.tensor_scalar(res1[:, g, :], u_rows[:], rs[:, g:g + 1], 0.0, ALU.mult, ALU.add)
                last.then_inc(res1_step, 1)
                pool.wait_ge(res1_step, 3 * i + 2)
                P.tensor_tensor(res1[:], res1[:], res1_b[:], ALU.add).then_inc(res1_step, 1)

            def residual2(s, j):
                pool.wait_ge(x1_ready, G * j + G)
                P.tensor_tensor(res2[:], x1[:], bo_rows[:].unsqueeze(1).broadcast_to([128, G, D]),
                                ALU.add).then_inc(res2_ready, 1)

            def subtract_max(s, j, g):
                pool.wait_ge(mx_ready, G * j + g + 1)
                P.tensor_tensor(sm[:, g, :, :, :], sm[:, g, :, :, :],
                                mx[:, g, :, :].unsqueeze(3).broadcast_to([128, QT, DT, C]), ALU.subtract).then_inc(sub_ready, 1)

            def emit(s):
                i, j, o = s.conv, s.attn, s.out
                conv, attn, out_ = i is not None, j is not None, o is not None
                if out_:
                    pool.wait_ge(z2_var_ready, o + 1)
                    inverse_root(z2_rstd[:], z2_var[:], z2_rstd_ready)
                if attn:
                    residual2(s, j)
                if conv:
                    residual1(s, i)
                if attn:
                    subtract_max(s, j, 0)
                    subtract_max(s, j, 1)
                if conv:
                    pool.wait_ge(r_var_ready, i + 1)
                    inverse_root(r_rstd[:], r_var[:], r_rstd_ready)
                if attn:
                    subtract_max(s, j, 2)
                    subtract_max(s, j, 3)
                for pair in (0, 1):
                    if conv:
                        pool.wait_ge(z1_var_ready, 2 * i + pair + 1)
                        inverse_root(z1_rstd[:, 2 * pair:2 * pair + 2], z1_var[:, 2 * pair:2 * pair + 2], z1_rstd_ready)

            sections(pool, emit)


_OUTS = [((128, 128, 256), 'float32')]


def kernel(**inputs):
    import numpy as _np
    import concourse.bacc as _bacc
    from concourse import mybir as _mybir
    from concourse.bass_utils import run_bass_kernel_spmd as _run

    nc = _bacc.Bacc("TRN2", target_bir_lowering=False, num_devices=1)
    p = {k.replace("L0_gnn_", "").replace("L1_gnn_", ""): _np.asarray(v) for k, v in inputs.items()}
    def columns(a):
        return a.reshape(-1, 128).T

    order = [("x", p["x"]), ("adj", p["adj"]), ("w1t", p["W1"].T), ("b1", p["b1"]), ("gamma", columns(p["gamma"])),
             ("beta", columns(p["beta"])), ("w2t", p["W2"].T), ("b2", p["b2"]), ("wqt", p["Wq"].T), ("bq", columns(p["bq"])),
             ("wkt", p["Wk"].T), ("bk", columns(p["bk"])), ("wvt", p["Wv"].T), ("bv", columns(p["bv"])), ("wot", p["Wo"].T), ("bo", p["bo"])]
    arrays, args = {}, []
    for name, a in order:
        a = _np.ascontiguousarray(a)
        arrays[f"in_{name}"] = a
        args.append(nc.dram_tensor(f"in_{name}", a.shape, _mybir.dt.from_np(a.dtype), kind="ExternalInput").ap())
    for i, (shape, dtype) in enumerate(_OUTS):
        args.append(nc.dram_tensor(f"out_{i}_dram", shape, _mybir.dt.from_np(_np.dtype(dtype)), kind="ExternalOutput").ap())
    gnn_kernel(nc, *args)
    r = _run(nc, [arrays], core_ids=[0])
    return r.results[0]["out_0_dram"]
```

```python
import math

import concourse.bass as bass
from concourse import mybir
from contextlib import ExitStack

F32 = mybir.dt.float32
F32R = mybir.dt.float32r
F16 = mybir.dt.float16
BF16 = mybir.dt.bfloat16
ALU = mybir.AluOpType
ACT = mybir.ActivationFunctionType
AX = mybir.AxisListType

EPS = 1e-5
TINY = 1.1754944e-38
P_SCALE_LOG2 = 10
V_SCALE = 64.0

FRONT = ["ht", "cols", "dnb", "s", "px0", "px1"]
BACK = ["a0", "a1", "a2", "a3", "pr0", "pr1", "pr2", "pr3", "o20", "o21"]
PROJ = ["xt0", "xt1", "q0", "q1", "k0", "k1", "v0", "v1"]
ATTN = ["pt00", "pt01", "pt10", "pt11", "c0", "c1", "pt20", "pt21", "pt30", "pt31", "c2", "c3",
        "ct0", "ct1", "y0", "y1"]
TILES = ["a0", "a1", "a2", "ht", "a3", "cols", "pt00", "pt01", "pt10", "pr0", "pr1", "pr2", "pr3", "pt11",
         "o20", "pt21", "pt20", "o21", "pt30", "c0", "dnb", "pt31", "c1", "s", "c2", "xt0", "xt1", "px0",
         "c3", "q0", "ct0", "ct1", "q1", "k0", "y0", "y1", "px1", "k1", "v0", "v1"]
LAST_TILES = ["pt00", "pt01", "pt10", "pt11", "pt20", "pt21", "c0", "pt30", "pt31", "c1", "c2", "c3",
              "ct0", "ct1", "y0", "y1"]
RING = 4


class Section:

    def __init__(self, front, back, proj, attn, first_use, shift, before):
        self.front, self.back, self.proj, self.attn = front, back, proj, attn
        self.first_use, self.shift = first_use, shift
        self.order = list(before)
        for tile in TILES if proj is not None or front is not None else LAST_TILES:
            group = front if tile in FRONT else back if tile in BACK else proj if tile in PROJ else attn
            if group is not None:
                self.order.append((tile, group))
        self.tiles = [tile for tile, _ in self.order[len(before):]]

    def bank(self, tile):
        return (self.shift + self.tiles.index(tile)) % RING

    def full(self, tile):
        return self.first_use + (self.shift + self.tiles.index(tile)) // RING + 1

    def before(self, tile):
        at = len(self.order) - len(self.tiles) + self.tiles.index(tile) - RING
        return self.order[at] if at >= 0 else None


def later(group):
    return not (isinstance(group, int) and group == 0)


def gnn_kernel(nc, x, adj, w1t, w2t, w_proj, b1, vec_cols, vec_rows, out):
    N, C, D = x.shape
    DH = w1t.shape[1]
    HEADS = 8
    HD = D // HEADS
    QSCALE = 2.0 * HD ** -0.5
    G = 4
    GROUPS = N // G
    DT, HT_ = D // C, DH // C
    QT = HEADS // DT

    ctx = ExitStack()
    with ctx:
        def sb(name, shape, dt=F32):
            return ctx.enter_context(nc.sbuf_tensor(name, shape, dt))

        def sem(name):
            return ctx.enter_context(nc.semaphore(name))

        ring = [ctx.enter_context(nc.psum_tensor(f"ring{b}", [128, 512], F32)) for b in range(RING)]
        scores = ctx.enter_context(nc.psum_tensor("scores", [128, QT, 2, DT, C], F32))

        ident_bf = sb("ident_bf", [128, 128], BF16)
        ident = sb("ident", [128, 128])
        ones_bf = sb("ones_bf", [128, 1], BF16)
        ones_r = sb("ones_r", [128, 128], F32R)
        mean_w = sb("mean_w", [128, 128])
        neg_half = sb("neg_half", [128, G])
        half = sb("half", [128, 1])
        p_bias = sb("p_bias", [128, 1])
        W1 = [sb(f"w1_{h}", [128, DT, DH], F32R) for h in ("hi", "lo")]
        W2 = [sb(f"w2_{h}", [128, HT_, D], F32R) for h in ("hi", "lo")]
        WQ = [sb(f"wq_{h}", [128, DT, D], F32R) for h in ("hi", "lo")]
        WK = [sb(f"wk_{h}", [128, DT, D], F32R) for h in ("hi", "lo")]
        WV = [sb(f"wv_{h}", [128, DT, D], F32R) for h in ("hi", "lo")]
        WO = [sb(f"wo_{h}", [128, DT, D], F32R) for h in ("hi", "lo")]
        b1_rows = sb("b1_rows", [128, DH], F32R)
        b1_row = sb("b1_row", [1, DH])
        vectors = sb("vectors", [128, 3 * DT + 2 * HT_])
        bias_cols = sb("bias_cols", [128, 2, DT])
        u_rows = sb("u_rows", [128, D])
        b_rows = sb("b_rows", [128, 2, D])
        b2_rows, bo_rows = b_rows[:, 0, :], b_rows[:, 1, :]
        v_norm = sb("v_norm", [128, 4])
        w_nat = sb("w_nat", [128, C])
        w_rest = sb("w_rest", [128, N])
        w_cols = sb("w_cols", [128, N, 4], BF16)

        x_in = sb("x_in", [128, G, D])
        adj_in = sb("adj_in", [128, G, C])
        H = sb("H", [128, G, C], BF16)
        HT = sb("HT", [128, G, C], BF16)
        wg = sb("wg", [128, G, 4], BF16)
        cd = sb("cd", [128, 2, G])
        rc = sb("rc", [128, G])
        cd_inv = sb("cd_inv", [128, 2, G])
        cd_rec = sb("cd_rec", [128, 2, G])
        cd_rest = sb("cd_rest", [128, 2, G])
        cd_part = sb("cd_part", [128, 3, 2, G], BF16)
        rs = sb("rs", [128, G])
        U = sb("U", [128, 3, G, C], BF16)
        dnb = sb("dnb", [128, G, C])
        PT = sb("PT", [128, G, C])
        PTr = sb("PTr", [128, G, C])
        px = [sb(f"px_{h}", [128, G, DT, C], F32R) for h in ("hi", "lo")]
        r = sb("r", [128, G, DH])
        r_stats = sb("r_stats", [128, G, 6])
        r_mv = sb("r_mv", [128, G, 2])
        r_var = sb("r_var", [128, G])
        r_rstd = sb("r_rstd", [128, G])
        pr = [sb(f"pr_{h}", [128, G, HT_, C], F32R) for h in ("hi", "lo")]
        res1 = sb("res1", [128, G, D])
        res1_b = sb("res1_b", [128, G, D])
        z1 = sb("z1", [128, G, D])
        z1_stats = sb("z1_stats", [128, G, 6])
        z1_mv = sb("z1_mv", [128, G, 2])
        z1_var = sb("z1_var", [128, G])
        z1_rstd = sb("z1_rstd", [128, G])
        x1 = sb("x1", [128, G, D])

        adj_mask = sb("adj_mask", [128, G, C])
        res2 = sb("res2", [128, G, D])
        xt = [sb(f"xt_{h}", [128, DT, G, C], F32R) for h in ("hi", "lo")]
        q = sb("q", [128, DT, G, C])
        k = sb("k", [128, DT, G, C])
        v = [sb(f"v_{h}", [128, G, HEADS, HD + 1], F16) for h in ("hi", "lo")]
        sm = sb("sm", [128, G, QT, DT, C])
        mx = sb("mx", [128, G, QT, DT])
        p_full = sb("p_full", [128, G, HEADS, C])
        pT = [sb(f"p_{h}", [128, G, HEADS, C], F16) for h in ("hi", "lo")]
        rinv = sb("rinv", [128, G, HEADS])
        cx = sb("cx", [128, G, D])
        ct = [sb(f"ct_{h}", [128, DT, G, C], F32R) for h in ("hi", "lo")]
        z2 = sb("z2", [128, G, D])
        z2_stats = sb("z2_stats", [128, G, 6])
        z2_mv = sb("z2_mv", [128, G, 2])
        z2_var = sb("z2_var", [128, G])
        z2_rstd = sb("z2_rstd", [128, G])
        y_out = sb("y_out", [128, G, D])

        bank_full = [sem(f"bank_full{b}") for b in range(RING)]
        scores_full = sem("scores_full")
        const_ready, edge_w_loaded, vectors_loaded, rows_loaded = (
            sem("const_ready"), sem("edge_w_loaded"), sem("vectors_loaded"), sem("rows_loaded"))
        w1_loaded, w2_loaded, proj_loaded = sem("w1_loaded"), sem("w2_loaded"), sem("proj_loaded")
        edge_w_turned, edge_w_step, products_in, products_ready = (
            sem("edge_w_turned"), sem("edge_w_step"), sem("products_in"), sem("products_ready"))
        bias_step, w1_hi, w1_ready, w2_step, w2_ready, rows_ready = (
            sem("bias_step"), sem("w1_hi"), sem("w1_ready"), sem("w2_step"), sem("w2_ready"), sem("rows_ready"))
        norm_step, norm_ready, v_scale_ready = sem("norm_step"), sem("norm_ready"), sem("v_scale_ready")
        proj_scaled, proj_hi, proj_ready = sem("proj_scaled"), sem("proj_hi"), sem("proj_ready")
        p_all, p_lo, v_hi = sem("p_all"), sem("p_lo"), sem("v_hi")
        x_loaded, adj_loaded, mask_loaded, stored = sem("x_loaded"), sem("adj_loaded"), sem("mask_loaded"), sem("stored")
        h_ready, ht_ready, wg_ready = sem("h_ready"), sem("ht_ready"), sem("wg_ready")
        cols_step, u_ready, dnb_ready, pt_ready, ptr_ready = (
            sem("cols_step"), sem("u_ready"), sem("dnb_ready"), sem("pt_ready"), sem("ptr_ready"))
        px_hi, px_lo, r_ready, pr_hi, pr_lo = sem("px_hi"), sem("px_lo"), sem("r_ready"), sem("pr_hi"), sem("pr_lo")
        r_stats_ready, r_mv_ready, r_var_ready, r_rstd_ready = (
            sem("r_stats_ready"), sem("r_mv_ready"), sem("r_var_ready"), sem("r_rstd_ready"))
        z1_ready, z1_stats_ready, z1_mv_ready = sem("z1_ready"), sem("z1_stats_ready"), sem("z1_mv_ready")
        res1_step, z1_var_ready, z1_rstd_ready, x1_ready = (
            sem("res1_step"), sem("z1_var_ready"), sem("z1_rstd_ready"), sem("x1_ready"))
        res2_ready, xt_hi, xt_lo = sem("res2_ready"), sem("xt_hi"), sem("xt_lo")
        qk_ready, v_ready = sem("qk_ready"), sem("v_ready")
        sm_ready, mx_ready, sub_ready = sem("sm_ready"), sem("mx_ready"), sem("sub_ready")
        rinv_ready, cx_ready, ct_hi, ct_lo = sem("rinv_ready"), sem("cx_ready"), sem("ct_hi"), sem("ct_lo")
        z2_ready, z2_stats_ready, z2_mv_ready = sem("z2_ready"), sem("z2_stats_ready"), sem("z2_mv_ready")
        r_stats_seen, z1_stats_seen, z2_stats_seen = sem("r_stats_seen"), sem("z1_stats_seen"), sem("z2_stats_seen")
        z2_var_ready, z2_rstd_ready, y_ready = (
            sem("z2_var_ready"), sem("z2_rstd_ready"), sem("y_ready"))

        x_g = x.rearrange("n c d -> c n d")
        adj_g = adj.rearrange("n c e -> c n e")
        out_g = out.rearrange("n c d -> c n d")
        w_in = p_full[:].rearrange("p g h c -> p (g h c)")
        w1_in = w_in[:, 0:DT * DH]
        w2_in = w_in[:, DT * DH:DT * DH + HT_ * D]
        proj_in = w_in[:, DT * DH + HT_ * D:].rearrange("p (m k) -> p m k", m=4)
        w2_gamma = sm[:, 0, :, :, :].rearrange("p a b c -> p (a b c)")
        v_squares = sm[:, 1, 0:2, :, :].rearrange("p a b c -> p (a b c)")
        bv_cols, gamma_cols, beta_cols = (
            vectors[:, 2 * DT:3 * DT], vectors[:, 3 * DT:3 * DT + HT_], vectors[:, 3 * DT + HT_:])
        prep_bank = [scores[:, b, :, :, :].rearrange("p g t c -> p (g t c)") for b in range(4)]
        COLS_STEPS = 11

        def sections(eng, emit, emit_last):
            tiles, last = 0, []

            def section(front, back, proj, attn):
                nonlocal tiles, last
                s = Section(front, back, proj, attn, tiles // RING, tiles % RING, last)
                tiles, last = tiles + len(s.tiles), s.order[-RING:]
                return s

            emit(section(0, None, None, None))
            emit(section(1, 0, 0, None))
            steps, uses = GROUPS - 2, len(TILES) // RING
            assert len(TILES) % RING == 0 and [tile for tile, _ in last] == TILES[-RING:]
            with eng.Fori(1, GROUPS - 1) as n:
                last = Section(n, n - 1, n - 1, n - 2, 0, 0, []).order[-RING:]
                emit(Section(n + 1, n, n, n - 1, (n - 1) * uses + tiles // RING, tiles % RING, last))
            tiles += steps * len(TILES)
            last = Section(GROUPS - 1, GROUPS - 2, GROUPS - 2, GROUPS - 3, 0, 0, []).order[-RING:]
            emit(section(None, GROUPS - 1, GROUPS - 1, GROUPS - 2))
            emit_last(section(None, None, None, GROUPS - 1))

        block = ctx.enter_context(nc.Block())

        @block.sync
        def _(sp):
            sp.dma_start(w_nat[0:N, :], adj[:, 0, :]).then_inc(edge_w_loaded, 16)
            sp.dma_start(adj_in[:], adj_g[:, 0:G, :]).then_inc(adj_loaded, 16)
            sp.dma_start(vectors[:], vec_cols).then_inc(vectors_loaded, 16)
            sp.dma_start(b1_row[:], b1.rearrange("(a n) -> a n", a=1)).then_inc(vectors_loaded, 16)
            sp.dma_start(x_in[:], x_g[:, 0:G, :]).then_inc(x_loaded, 16)
            sp.dma_start(w1_in.rearrange("p (t n) -> p t n", t=DT),
                         w1t.rearrange("(t p) n -> p t n", p=128)).then_inc(w1_loaded, 16)
            sp.dma_start(w2_in.rearrange("p (t n) -> p t n", t=HT_),
                         w2t.rearrange("(t p) n -> p t n", p=128)).then_inc(w2_loaded, 16)
            sp.dma_start(proj_in.rearrange("p m (t n) -> p (m t) n", t=DT),
                         w_proj.rearrange("m (t p) n -> p (m t) n", p=128)).then_inc(proj_loaded, 16)
            sp.dma_start(b_rows[:].rearrange("p a n -> p (a n)"),
                         vec_rows.rearrange("(a n) -> a n", a=1).partition_broadcast(128)).then_inc(rows_loaded, 16)
            sp.dma_start(adj_mask[:], adj_g[:, 0:G, :]).then_inc(mask_loaded, 16)

            def emit(s):
                f, j = s.front, s.attn
                if f is not None and later(f):
                    sp.wait_ge(h_ready, f)
                    sp.dma_start(adj_in[:], adj_g[:, bass.ds(f * G, G), :]).then_inc(adj_loaded, 16)
                    sp.wait_ge(px_hi, 2 * f)
                    sp.wait_ge(res1_step, 4 * f)
                    sp.dma_start(x_in[:], x_g[:, bass.ds(f * G, G), :]).then_inc(x_loaded, 16)
                if j is not None:
                    sp.wait_ge(sm_ready, G * j + G)
                    if s.back is not None:
                        sp.dma_start(adj_mask[:], adj_g[:, bass.ds(j * G + G, G), :]).then_inc(mask_loaded, 16)
                    sp.wait_ge(y_ready, G * j + G)
                    sp.dma_start(out_g[:, bass.ds(j * G, G), :], y_out[:]).then_inc(stored, 16)

            sections(sp, emit, emit)
            sp.wait_ge(stored, 16 * GROUPS + 16)

        @block.tensor
        def _(pe):
            mm = nc.tensor.matmul

            released = {
                "ht": lambda i: (ht_ready, i + 1),
                "cols": lambda i: (cols_step, COLS_STEPS * i + 3),
                "dnb": lambda i: (dnb_ready, i + 1),
                "s": lambda i: (pt_ready, i + 1),
            }
            for g in range(G):
                released[f"a{g}"] = lambda i, g=g: (r_ready, G * i + g + 1)
                released[f"pr{g}"] = lambda i, g=g: (pr_lo, G * i + g + 1)
                released[f"c{g}"] = lambda i, g=g: (cx_ready, G * i + g + 1)
                for t in range(DT):
                    released[f"pt{g}{t}"] = lambda i, g=g, t=t: (p_all, DT * (G * i + g) + t + 1)
            for p in range(2):
                released[f"px{p}"] = lambda i, p=p: (px_lo, 2 * i + p + 1)
                released[f"o2{p}"] = lambda i, p=p: (z1_ready, 2 * i + p + 1)
                released[f"xt{p}"] = lambda i, p=p: (xt_lo, 2 * i + p + 1)
                released[f"q{p}"] = lambda i, p=p: (qk_ready, 4 * i + p + 1)
                released[f"k{p}"] = lambda i, p=p: (qk_ready, 4 * i + p + 3)
                released[f"v{p}"] = lambda i, p=p: (v_ready, 2 * i + p + 1)
                released[f"ct{p}"] = lambda i, p=p: (ct_lo, 2 * i + p + 1)
                released[f"y{p}"] = lambda i, p=p: (z2_ready, 2 * i + p + 1)

            def claim(s, tile):
                if s.before(tile):
                    tile_before, group = s.before(tile)
                    done, count = released[tile_before](group)
                    pe.wait_ge(done, count)
                return ring[s.bank(tile)]

            def split_product(dst, lhs, rhs, extra=None):
                (a_hi, a_lo), (b_hi, b_lo) = lhs, rhs
                n = len(a_hi)
                pairs = [(a_hi[t], b_hi[t]) for t in range(n)] + [(a_hi[t], b_lo[t]) for t in range(n)]
                pairs += [(a_lo[t], b_hi[t]) for t in range(n)]
                if extra:
                    pairs = [extra] + pairs
                for m, (a, b) in enumerate(pairs):
                    last = mm(dst, a, b, start=(m == 0), stop=(m == len(pairs) - 1))
                return last

            pe.wait_ge(const_ready, 10)
            pe.wait_ge(edge_w_loaded, 16)
            nc.tensor.transpose(prep_bank[0][:, 0:N], w_nat[0:N, :], ident[0:N, 0:N]).then_inc(edge_w_turned, 1)

            def weight_products():
                pe.wait_ge(products_in, 5)
                pe.wait_ge(edge_w_step, 6)
                mm(prep_bank[0][:], mean_w[:], v_squares, start=True, stop=True)
                for t in range(HT_):
                    mm(prep_bank[1][:, 0:D], mean_w[:], w2_gamma[:, t * D:(t + 1) * D], start=t == 0, stop=t == HT_ - 1)
                for t in range(HT_):
                    mm(prep_bank[2][:, 0:D], beta_cols[:, t:t + 1].broadcast_to([128, 128]),
                       w2_in[:, t * D:(t + 1) * D], start=t == 0, stop=t == HT_ - 1)
                for t in range(DT):
                    last = mm(prep_bank[3][:, 0:D], bv_cols[:, t:t + 1].broadcast_to([128, 128]),
                              proj_in[:, 3, t * D:(t + 1) * D], start=t == 0, stop=t == DT - 1)
                last.then_inc(products_ready, 1)

            def incidence_transposed(s, i):
                bank = claim(s, "ht")
                pe.wait_ge(h_ready, i + 1)
                dst = bank[:, 0:G * C // 2].bitcast(BF16)
                for g in range(G):
                    last = nc.tensor.transpose(dst[:, g * C:(g + 1) * C], H[:, g, :], ident_bf[:])
                last.then_inc(bank_full[s.bank("ht")], 1)

            def degree_columns(s, i):
                bank = claim(s, "cols")
                pe.wait_ge(ht_ready, i + 1)
                pe.wait_ge(wg_ready, i + 1)
                for g in range(G):
                    mm(bank[:, 8 * g:8 * g + 4], HT[:, g, :], wg[:, g, :], start=True, stop=True)
                    last = mm(bank[:, 8 * g + 4:8 * g + 5], H[:, g, :], ones_bf[:], start=True, stop=True)
                last.then_inc(bank_full[s.bank("cols")], 1)

            def degree_rows(s, i):
                bank = claim(s, "dnb")
                pe.wait_ge(cols_step, COLS_STEPS * i + COLS_STEPS)
                for g in range(G):
                    for m in range(3):
                        last = mm(bank[:, g * C:(g + 1) * C], cd_part[:, m, 1, g:g + 1].broadcast_to([128, 128]),
                                  ident_bf[:], start=m == 0, stop=m == 2)
                last.then_inc(bank_full[s.bank("dnb")], 1)

            def shared_edges(s, i):
                bank = claim(s, "s")
                pe.wait_ge(u_ready, 3 * i + 3)
                for g in range(G):
                    for m in range(3):
                        last = mm(bank[:, g * C:(g + 1) * C], HT[:, g, :], U[:, m, g, :], start=m == 0, stop=m == 2)
                last.then_inc(bank_full[s.bank("s")], 1)

            def propagate_x(s, i, pair):
                tile = f"px{pair}"
                bank = claim(s, tile)
                pe.wait_ge(pt_ready, i + 1)
                pe.wait_ge(x_loaded, 16 * i + 16)
                for g in (0, 1):
                    for t in range(DT):
                        at = (g * DT + t) * C
                        last = mm(bank[:, at:at + C], x_in[:, 2 * pair + g, t * C:(t + 1) * C], PT[:, 2 * pair + g, :],
                                  start=True, stop=True)
                last.then_inc(bank_full[s.bank(tile)], 1)

            def hidden(s, i, g):
                tile = f"a{g}"
                bank = claim(s, tile)
                pe.wait_ge(px_lo, 2 * i + g // 2 + 1)
                if not later(i):
                    pe.wait_ge(w1_ready, 2)
                split_product(bank[:], [[p[:, g, t, :] for t in range(DT)] for p in px],
                              [[w[:, t, :] for t in range(DT)] for w in W1],
                              extra=(ones_r[:], b1_rows[:])).then_inc(bank_full[s.bank(tile)], 1)

            def propagate_r(s, i, g):
                tile = f"pr{g}"
                bank = claim(s, tile)
                pe.wait_ge(ptr_ready, i + 1)
                for t in range(HT_):
                    last = mm(bank[:, t * C:(t + 1) * C], r[:, g, t * C:(t + 1) * C], PTr[:, g, :], start=True, stop=True)
                last.then_inc(bank_full[s.bank(tile)], 1)

            def second_conv(s, i, pair):
                tile = f"o2{pair}"
                bank = claim(s, tile)
                if not later(i):
                    pe.wait_ge(w2_ready, 1)
                for g in (0, 1):
                    pe.wait_ge(pr_lo, G * i + 2 * pair + g + 1)
                    last = split_product(bank[:, g * D:(g + 1) * D],
                                         [[p[:, 2 * pair + g, t, :] for t in range(HT_)] for p in pr],
                                         [[w[:, t, :] for t in range(HT_)] for w in W2])
                last.then_inc(bank_full[s.bank(tile)], 1)

            def x1_transposed(s, j, t):
                tile = f"xt{t}"
                bank = claim(s, tile)
                pe.wait_ge(x1_ready, G * j + G)
                for g in range(G):
                    last = nc.tensor.transpose(bank[:, g * C:(g + 1) * C], x1[:, g, t * C:(t + 1) * C], ident[:])
                last.then_inc(bank_full[s.bank(tile)], 1)

            def queries_keys(s, j, name, weights, f):
                tile = f"{name}{f}"
                bank = claim(s, tile)
                if not later(j):
                    pe.wait_ge(proj_ready, 2)
                pe.wait_ge(xt_lo, 2 * j + 2)
                split_product(bank[:], [[w[:, t, f * C:(f + 1) * C] for t in range(DT)] for w in weights],
                              [[a[:, t, :, :].rearrange("p g c -> p (g c)") for t in range(DT)] for a in xt]
                              ).then_inc(bank_full[s.bank(tile)], 1)

            def values(s, j, pair):
                tile = f"v{pair}"
                bank = claim(s, tile)
                if not later(j):
                    pe.wait_ge(proj_ready, 4)
                pe.wait_ge(xt_lo, 2 * j + 2)
                for g in (0, 1):
                    last = split_product(bank[:, g * D:(g + 1) * D],
                                         [[a[:, t, 2 * pair + g, :] for t in range(DT)] for a in xt],
                                         [[w[:, t, :] for t in range(DT)] for w in WV])
                last.then_inc(bank_full[s.bank(tile)], 1)

            def score_pair(s, j, pair):
                pe.wait_ge(qk_ready, 4 * j + 4)
                if pair == 1:
                    pe.wait_ge(sm_ready, G * j + 2)
                elif later(j):
                    pe.wait_ge(sm_ready, G * j)
                for g in (0, 1):
                    for t in range(DT):
                        for h in range(QT):
                            rows = slice(h * HD, (h + 1) * HD)
                            last = mm(scores[:, h, g, t, :], q[rows, t, 2 * pair + g, :], k[rows, t, 2 * pair + g, :],
                                      start=True, stop=True)
                last.then_inc(scores_full, 1)

            def scores_transposed(s, j, g, t):
                tile = f"pt{g}{t}"
                bank = claim(s, tile)
                pe.wait_ge(sub_ready, G * j + g + 1)
                for h in range(QT):
                    last = nc.tensor.transpose(bank[:, h * C:(h + 1) * C], sm[:, g, h, t, :], ident[:])
                last.then_inc(bank_full[s.bank(tile)], 1)

            def context(s, j, g):
                tile = f"c{g}"
                bank = claim(s, tile)
                pe.wait_ge(p_lo, G * j + g + 1)
                pe.wait_ge(v_ready, 2 * j + 2)
                for h in range(HEADS):
                    for m, (a, b) in enumerate(((0, 0), (0, 1), (1, 0))):
                        last = mm(bank[:, h * (HD + 1):(h + 1) * (HD + 1)], pT[a][:, g, h, :], v[b][:, g, h, :],
                                  start=m == 0, stop=m == 2)
                last.then_inc(bank_full[s.bank(tile)], 1)

            def context_transposed(s, j, t):
                tile = f"ct{t}"
                bank = claim(s, tile)
                pe.wait_ge(cx_ready, G * j + G)
                for g in range(G):
                    last = nc.tensor.transpose(bank[:, g * C:(g + 1) * C], cx[:, g, t * C:(t + 1) * C], ident[:])
                last.then_inc(bank_full[s.bank(tile)], 1)

            def output(s, j, pair):
                tile = f"y{pair}"
                bank = claim(s, tile)
                pe.wait_ge(ct_lo, 2 * j + 2)
                for g in (0, 1):
                    last = split_product(bank[:, g * D:(g + 1) * D],
                                         [[a[:, t, 2 * pair + g, :] for t in range(DT)] for a in ct],
                                         [[w[:, t, :] for t in range(DT)] for w in WO])
                last.then_inc(bank_full[s.bank(tile)], 1)

            def emit(s):
                f, b, p, j = s.front, s.back, s.proj, s.attn
                front, back, proj, attn = (n is not None for n in (f, b, p, j))
                if back:
                    hidden(s, b, 0)
                    hidden(s, b, 1)
                    hidden(s, b, 2)
                if front:
                    incidence_transposed(s, f)
                if back:
                    hidden(s, b, 3)
                if front:
                    degree_columns(s, f)
                if back and not later(b):
                    weight_products()
                if attn:
                    scores_transposed(s, j, 0, 0)
                    score_pair(s, j, 1)
                    scores_transposed(s, j, 0, 1)
                    scores_transposed(s, j, 1, 0)
                if back:
                    propagate_r(s, b, 0)
                    propagate_r(s, b, 1)
                    propagate_r(s, b, 2)
                    propagate_r(s, b, 3)
                if attn:
                    scores_transposed(s, j, 1, 1)
                if back:
                    second_conv(s, b, 0)
                if attn:
                    scores_transposed(s, j, 2, 1)
                    scores_transposed(s, j, 2, 0)
                if back:
                    second_conv(s, b, 1)
                if attn:
                    scores_transposed(s, j, 3, 0)
                    context(s, j, 0)
                if front:
                    degree_rows(s, f)
                if attn:
                    scores_transposed(s, j, 3, 1)
                    context(s, j, 1)
                if front:
                    shared_edges(s, f)
                if attn:
                    context(s, j, 2)
                if proj:
                    x1_transposed(s, p, 0)
                    x1_transposed(s, p, 1)
                if front:
                    propagate_x(s, f, 0)
                if attn:
                    context(s, j, 3)
                if proj:
                    queries_keys(s, p, "q", WQ, 0)
                if attn:
                    context_transposed(s, j, 0)
                    context_transposed(s, j, 1)
                if proj:
                    queries_keys(s, p, "q", WQ, 1)
                    queries_keys(s, p, "k", WK, 0)
                if attn:
                    output(s, j, 0)
                    output(s, j, 1)
                if front:
                    propagate_x(s, f, 1)
                if proj:
                    queries_keys(s, p, "k", WK, 1)
                    values(s, p, 0)
                    values(s, p, 1)
                    score_pair(s, p, 0)

            def emit_last(s):
                j = s.attn
                score_pair(s, j, 1)
                scores_transposed(s, j, 0, 0)
                scores_transposed(s, j, 0, 1)
                scores_transposed(s, j, 1, 0)
                scores_transposed(s, j, 1, 1)
                scores_transposed(s, j, 2, 0)
                scores_transposed(s, j, 2, 1)
                context(s, j, 0)
                scores_transposed(s, j, 3, 0)
                scores_transposed(s, j, 3, 1)
                context(s, j, 1)
                context(s, j, 2)
                context(s, j, 3)
                context_transposed(s, j, 0)
                context_transposed(s, j, 1)
                output(s, j, 0)
                output(s, j, 1)

            sections(pe, emit, emit_last)

        @block.scalar
        def _(act):
            def filled(s, tile):
                act.wait_ge(bank_full[s.bank(tile)], s.full(tile))
                return ring[s.bank(tile)]

            def copy(dst, src):
                return nc.scalar.activation(dst, src, ACT.Copy)

            act.wait_ge(w1_loaded, 16)
            copy(W1[0][:].rearrange("p t n -> p (t n)"), w1_in).then_inc(w1_hi, 1)

            def projection_halves():
                act.wait_ge(proj_scaled, 3)
                for n, w in enumerate((WQ, WK, WV, WO)):
                    copy(w[0][:].rearrange("p t n -> p (t n)"), proj_in[:, n, :]).then_inc(proj_hi, 1)

            def incidence_transposed(s, i):
                bank = filled(s, "ht")
                copy(HT[:].rearrange("p g c -> p (g c)"), bank[:, 0:G * C // 2].bitcast(BF16)).then_inc(ht_ready, 1)

            def degree_rows(s, i):
                bank = filled(s, "dnb")
                copy(dnb[:].rearrange("p g c -> p (g c)"), bank[:]).then_inc(dnb_ready, 1)

            def px_high(s, i, pair):
                bank = filled(s, f"px{pair}")
                copy(px[0][:, 2 * pair:2 * pair + 2, :, :].rearrange("p g t c -> p (g t c)"), bank[:]).then_inc(px_hi, 1)

            def relu(s, i, g):
                bank = filled(s, f"a{g}")
                if later(i):
                    act.wait_ge(r_stats_ready, G * i - G + g + 1)
                nc.scalar.activation(r[:, g, :], bank[:], ACT.Relu).then_inc(r_ready, 1)

            def pr_high(s, i, g):
                bank = filled(s, f"pr{g}")
                copy(pr[0][:, g, :, :].rearrange("p t c -> p (t c)"), bank[:]).then_inc(pr_hi, 1)

            def xt_high(s, j, t):
                bank = filled(s, f"xt{t}")
                copy(xt[0][:, t, :, :].rearrange("p g c -> p (g c)"), bank[:]).then_inc(xt_hi, 1)

            def queries_keys(s, j, name, dst, bias, f):
                bank = filled(s, f"{name}{f}")
                nc.scalar.activation(dst[:, f, :, :].rearrange("p g c -> p (g c)"), bank[:], ACT.Identity,
                                     bias=bias_cols[:, bias, f:f + 1]).then_inc(qk_ready, 1)

            def values(s, j, pair):
                bank = filled(s, f"v{pair}")
                copy(v[0][:, 2 * pair:2 * pair + 2, :, 0:HD],
                     bank[:].rearrange("p (g h d) -> p g h d", g=2, h=HEADS)).then_inc(v_hi, 1)

            def exponential(s, j, g, t):
                bank = filled(s, f"pt{g}{t}")
                nc.scalar.activation(pT[0][:, g, t * QT:(t + 1) * QT, :].rearrange("p h c -> p (h c)"), bank[:],
                                     ACT.Exp, bias=p_bias[:])

            def exponential_full(s, j, g, t):
                bank = ring[s.bank(f"pt{g}{t}")]
                nc.scalar.activation(p_full[:, g, t * QT:(t + 1) * QT, :].rearrange("p h c -> p (h c)"), bank[:],
                                     ACT.Exp, bias=p_bias[:]).then_inc(p_all, 1)

            def ct_high(s, j, t):
                bank = filled(s, f"ct{t}")
                copy(ct[0][:, t, :, :].rearrange("p g c -> p (g c)"), bank[:]).then_inc(ct_hi, 1)

            def emit(s):
                f, b, p, j = s.front, s.back, s.proj, s.attn
                front, back, proj, attn = (n is not None for n in (f, b, p, j))
                if back:
                    relu(s, b, 0)
                    relu(s, b, 1)
                    relu(s, b, 2)
                if front:
                    incidence_transposed(s, f)
                if back:
                    relu(s, b, 3)
                if attn:
                    exponential(s, j, 0, 0)
                    exponential_full(s, j, 0, 0)
                    exponential(s, j, 0, 1)
                    exponential_full(s, j, 0, 1)
                    exponential(s, j, 1, 0)
                if back:
                    pr_high(s, b, 0)
                if attn:
                    exponential_full(s, j, 1, 0)
                if back:
                    pr_high(s, b, 1)
                    pr_high(s, b, 2)
                if attn:
                    exponential(s, j, 1, 1)
                if back:
                    pr_high(s, b, 3)
                if back and not later(b):
                    projection_halves()
                if attn:
                    exponential_full(s, j, 1, 1)
                    exponential(s, j, 2, 1)
                    exponential(s, j, 2, 0)
                    exponential_full(s, j, 2, 0)
                    exponential_full(s, j, 2, 1)
                    exponential(s, j, 3, 0)
                    exponential_full(s, j, 3, 0)
                if front:
                    degree_rows(s, f)
                if attn:
                    exponential(s, j, 3, 1)
                    exponential_full(s, j, 3, 1)
                if proj:
                    xt_high(s, p, 0)
                    xt_high(s, p, 1)
                if front:
                    px_high(s, f, 0)
                if attn:
                    ct_high(s, j, 0)
                if proj:
                    queries_keys(s, p, "q", q, 0, 0)
                if attn:
                    ct_high(s, j, 1)
                if proj:
                    queries_keys(s, p, "q", q, 0, 1)
                    queries_keys(s, p, "k", k, 1, 0)
                if front:
                    px_high(s, f, 1)
                if proj:
                    queries_keys(s, p, "k", k, 1, 1)
                    values(s, p, 0)
                    values(s, p, 1)

            def emit_last(s):
                j = s.attn
                exponential(s, j, 0, 0)
                exponential_full(s, j, 0, 0)
                exponential(s, j, 0, 1)
                exponential_full(s, j, 0, 1)
                exponential(s, j, 1, 0)
                exponential_full(s, j, 1, 0)
                exponential(s, j, 1, 1)
                exponential_full(s, j, 1, 1)
                exponential(s, j, 2, 0)
                exponential_full(s, j, 2, 0)
                exponential(s, j, 2, 1)
                exponential_full(s, j, 2, 1)
                exponential(s, j, 3, 0)
                exponential_full(s, j, 3, 0)
                exponential(s, j, 3, 1)
                exponential_full(s, j, 3, 1)
                ct_high(s, j, 0)
                ct_high(s, j, 1)

            sections(act, emit, emit_last)



        @block.vector
        def _(dve):
            V = nc.vector

            def filled(s, tile):
                dve.wait_ge(bank_full[s.bank(tile)], s.full(tile))
                return ring[s.bank(tile)]

            V.memset(w_cols[:], 1.0).then_inc(edge_w_step, 1)
            V.memset(b1_rows[:].bitcast(F32), 0.0).then_inc(bias_step, 1)
            V.memset(v[0][:], 1.0).then_inc(bias_step, 1)
            V.memset(v[1][:], 0.0).then_inc(bias_step, 1)
            dve.wait_ge(edge_w_turned, 1)
            dve.wait_ge(edge_w_step, 1)
            V.tensor_copy(w_cols[:, :, 0], prep_bank[0][:, 0:N]).then_inc(edge_w_step, 1)
            dve.wait_ge(edge_w_step, 2)
            V.tensor_tensor(w_rest[:], prep_bank[0][:, 0:N], w_cols[:, :, 0], ALU.subtract).then_inc(edge_w_step, 1)
            V.tensor_tensor(w_cols[:, :, 1], prep_bank[0][:, 0:N], w_cols[:, :, 0], ALU.subtract).then_inc(edge_w_step, 1)
            dve.wait_ge(edge_w_step, 4)
            V.tensor_tensor(w_cols[:, :, 2], w_rest[:], w_cols[:, :, 1], ALU.subtract).then_inc(edge_w_step, 1)
            dve.wait_ge(edge_w_step, 5)
            dve.sem_inc(edge_w_step, 1)

            def biases():
                dve.wait_ge(vectors_loaded, 32)
                dve.wait_ge(bias_step, 3)
                V.tensor_copy(b1_rows[0:1, :], b1_row[:]).then_inc(bias_step, 1)
                V.tensor_scalar(bias_cols[:, 0, :], vectors[:, 0:DT], QSCALE, None, ALU.mult).then_inc(bias_step, 1)
                V.tensor_copy(bias_cols[:, 1, :], vectors[:, DT:2 * DT]).then_inc(bias_step, 1)
                dve.wait_ge(bias_step, 6)
                V.tensor_tensor(b1_rows[32:33, :], b1_row[:], b1_rows[0:1, :].bitcast(F32), ALU.subtract).then_inc(w1_ready, 1)

            def row_constants():
                dve.wait_ge(products_ready, 1)
                V.tensor_copy(u_rows[:], prep_bank[2][:, 0:D]).then_inc(rows_ready, 1)
                dve.wait_ge(rows_loaded, 16)
                V.tensor_tensor(bo_rows, bo_rows, prep_bank[3][:, 0:D], ALU.add).then_inc(rows_ready, 1)
                V.tensor_reduce(v_norm[:, 0:1], prep_bank[0][:], AX.X, ALU.add).then_inc(norm_step, 1)
                dve.wait_ge(norm_step, 1)
                V.tensor_scalar(v_norm[:, 1:2], v_norm[:, 0:1], TINY, None, ALU.max).then_inc(norm_ready, 1)

            def centred_weights():
                for t in range(HT_):
                    V.tensor_tensor(w2_gamma[:, t * D:(t + 1) * D], w2_gamma[:, t * D:(t + 1) * D], prep_bank[1][:, 0:D],
                                    ALU.subtract).then_inc(w2_step, 1)
                dve.wait_ge(w2_step, HT_)
                V.tensor_copy(W2[0][:].rearrange("p t n -> p (t n)"), w2_gamma).then_inc(w2_step, 1)
                dve.wait_ge(w2_step, HT_ + 1)
                V.tensor_tensor(W2[1][:].rearrange("p t n -> p (t n)"), w2_gamma,
                                W2[0][:].rearrange("p t n -> p (t n)").bitcast(F32), ALU.subtract).then_inc(w2_ready, 1)

            def projections_low():
                for n, w in enumerate((WQ, WK, WV, WO)):
                    dve.wait_ge(proj_hi, n + 1)
                    V.tensor_tensor(w[1][:].rearrange("p t n -> p (t n)"), proj_in[:, n, :],
                                    w[0][:].rearrange("p t n -> p (t n)").bitcast(F32), ALU.subtract).then_inc(proj_ready, 1)

            def incidence(i):
                dve.wait_ge(adj_loaded, 16 * i + 16)
                V.tensor_scalar(H[:], adj_in[:], 0.0, None, ALU.not_equal).then_inc(h_ready, 1)
                V.tensor_copy(wg[:], w_cols[:, bass.ds(i * G, G), :]).then_inc(wg_ready, 1)

            def degrees(s, i):
                bank = filled(s, "cols")
                cols = bank[:, 0:8 * G].rearrange("p (g m) -> p g m", m=8)
                V.tensor_copy(cd[:, 0, :], cols[:, :, 4]).then_inc(cols_step, 1)
                V.tensor_copy(rc[:], cols[:, :, 3]).then_inc(cols_step, 1)
                V.tensor_reduce(cd[:, 1, :], cols[:, :, 0:3], AX.X, ALU.add).then_inc(cols_step, 1)
                dve.wait_ge(cols_step, COLS_STEPS * i + 3)
                V.tensor_scalar(cd_inv[:], cd[:], TINY, None, ALU.max).then_inc(cols_step, 1)

            def reciprocals(s, i):
                dve.wait_ge(cols_step, COLS_STEPS * i + 4)
                V.reciprocal(cd_rest[:], cd_inv[:]).then_inc(cols_step, 1)
                dve.wait_ge(cols_step, COLS_STEPS * i + 5)
                V.scalar_tensor_tensor(out=cd_rec[:], in0=cd[:], scalar=0.0, in1=cd_rest[:],
                                       op0=ALU.is_gt, op1=ALU.mult).then_inc(cols_step, 1)
                dve.wait_ge(cols_step, COLS_STEPS * i + 6)
                V.tensor_copy(cd_part[:, 0, :, :], cd_rec[:]).then_inc(cols_step, 1)

            def second_parts(s, i):
                if later(i):
                    dve.wait_ge(res1_step, 4 * i - 2)
                dve.wait_ge(cols_step, COLS_STEPS * i + 7)
                V.tensor_tensor(cd_inv[:], cd_rec[:], cd_part[:, 0, :, :], ALU.subtract).then_inc(cols_step, 1)
                V.tensor_tensor(cd_part[:, 1, :, :], cd_rec[:], cd_part[:, 0, :, :], ALU.subtract).then_inc(cols_step, 1)
                V.tensor_tensor(rs[:], cd_rec[:, 1, :], rc[:], ALU.mult).then_inc(cols_step, 1)

            def third_parts(s, i):
                dve.wait_ge(cols_step, COLS_STEPS * i + 9)
                V.tensor_tensor(cd_part[:, 2, :, :], cd_inv[:], cd_part[:, 1, :, :], ALU.subtract).then_inc(cols_step, 1)

            def edge_weights(s, i, m):
                dve.wait_ge(cols_step, COLS_STEPS * i + (7, 9, 11)[m])
                V.tensor_tensor(U[:, m, :, :], HT[:],
                                cd_part[:, m, 0, :].unsqueeze(2).broadcast_to([128, G, C]), ALU.mult).then_inc(u_ready, 1)

            def propagator(s, i):
                bank = filled(s, "s")
                dve.wait_ge(dnb_ready, i + 1)
                V.tensor_tensor(PT[:].rearrange("p g c -> p (g c)"), bank[:],
                                dnb[:].rearrange("p g c -> p (g c)"), ALU.mult).then_inc(pt_ready, 1)

            def low_half(s, tile, halves, hi_sem, lo_sem, value):
                bank = ring[s.bank(tile)]
                dve.wait_ge(hi_sem, value)
                V.tensor_tensor(halves[1], bank[:], halves[0].bitcast(F32), ALU.subtract).then_inc(lo_sem, 1)

            def px_low(s, i, pair):
                low_half(s, f"px{pair}", [p[:, 2 * pair:2 * pair + 2, :, :].rearrange("p g t c -> p (g t c)") for p in px],
                         px_hi, px_lo, 2 * i + pair + 1)

            def hidden_stats(s, i, g):
                dve.wait_ge(r_ready, G * i + g + 1)
                V.bn_stats(r_stats[:, g, :], r[:, g, :]).then_inc(r_stats_ready, 1)

            def hidden_variance(s, i):
                dve.wait_ge(r_stats_ready, G * i + G)
                dve.sem_inc(r_stats_seen, 1)
                for g in range(G):
                    V.bn_aggr(r_mv[:, g, :], r_stats[:, g, :]).then_inc(r_mv_ready, 1)
                dve.wait_ge(r_mv_ready, G * i + G)
                V.tensor_scalar(r_var[:], r_mv[:, :, 1], EPS, None, ALU.add).then_inc(r_var_ready, 1)

            def scaled_propagator(s, i):
                dve.wait_ge(pt_ready, i + 1)
                dve.wait_ge(r_rstd_ready, i + 1)
                V.tensor_tensor(PTr[:], PT[:], r_rstd[:].unsqueeze(2).broadcast_to([128, G, C]),
                                ALU.mult).then_inc(ptr_ready, 1)

            def pr_low(s, i, g):
                low_half(s, f"pr{g}", [p[:, g, :, :].rearrange("p t c -> p (t c)") for p in pr], pr_hi, pr_lo, G * i + g + 1)

            def residual_add(s, i, pair):
                bank = filled(s, f"o2{pair}")
                dve.wait_ge(res1_step, 4 * i + 4)
                two = slice(2 * pair, 2 * pair + 2)
                V.tensor_tensor(z1[:, two, :].rearrange("p g d -> p (g d)"), bank[:],
                                res1[:, two, :].rearrange("p g d -> p (g d)"), ALU.add).then_inc(z1_ready, 1)

            def residual_stats(i, pair):
                dve.wait_ge(z1_ready, 2 * i + pair + 1)
                for g in (2 * pair, 2 * pair + 1):
                    V.bn_stats(z1_stats[:, g, :], z1[:, g, :]).then_inc(z1_stats_ready, 1)

            def residual_variance(i, pair):
                two = slice(2 * pair, 2 * pair + 2)
                dve.wait_ge(z1_stats_ready, G * i + 2 * pair + 2)
                dve.sem_inc(z1_stats_seen, 1)
                for g in (2 * pair, 2 * pair + 1):
                    V.bn_aggr(z1_mv[:, g, :], z1_stats[:, g, :]).then_inc(z1_mv_ready, 1)
                dve.wait_ge(z1_mv_ready, G * i + 2 * pair + 2)
                V.tensor_scalar(z1_var[:, two], z1_mv[:, two, 1], EPS, None, ALU.add).then_inc(z1_var_ready, 1)

            def output_residual(s, o, pair):
                bank = filled(s, f"y{pair}")
                dve.wait_ge(res2_ready, o + 1)
                two = slice(2 * pair, 2 * pair + 2)
                V.tensor_tensor(z2[:, two, :].rearrange("p g d -> p (g d)"), bank[:],
                                res2[:, two, :].rearrange("p g d -> p (g d)"), ALU.add).then_inc(z2_ready, 1)

            def output_stats(o):
                dve.wait_ge(z2_ready, 2 * o + 2)
                for g in range(G):
                    V.bn_stats(z2_stats[:, g, :], z2[:, g, :]).then_inc(z2_stats_ready, 1)

            def output_variance(o):
                dve.wait_ge(z2_stats_ready, G * o + G)
                dve.sem_inc(z2_stats_seen, 1)
                for g in range(G):
                    V.bn_aggr(z2_mv[:, g, :], z2_stats[:, g, :]).then_inc(z2_mv_ready, 1)
                dve.wait_ge(z2_mv_ready, G * o + G)
                V.tensor_scalar(z2_var[:], z2_mv[:, :, 1], EPS, None, ALU.add).then_inc(z2_var_ready, 1)

            def normalise(ready, graphs, rstd_value, dst, z, mv, rstd, rstd_ready):
                dve.wait_ge(rstd_ready, rstd_value)
                for g in graphs:
                    V.tensor_scalar(dst[:, g, :], z[:, g, :], mv[:, g, 0:1], rstd[:, g:g + 1],
                                    ALU.subtract, ALU.mult).then_inc(ready, 1)

            def xt_low(s, j, t):
                low_half(s, f"xt{t}", [a[:, t, :, :].rearrange("p g c -> p (g c)") for a in xt], xt_hi, xt_lo, 2 * j + t + 1)

            def exponentials_low(j, g):
                dve.wait_ge(p_all, DT * (G * j + g + 1))
                V.tensor_tensor(pT[1][:, g, :, :], p_full[:, g, :, :], pT[0][:, g, :, :], ALU.subtract).then_inc(p_lo, 1)

            def values_low(s, j, pair):
                dve.wait_ge(v_hi, 2 * j + pair + 1)
                two = slice(2 * pair, 2 * pair + 2)
                V.tensor_tensor(v[1][:, two, :, 0:HD],
                                ring[s.bank(f"v{pair}")][:].rearrange("p (g h d) -> p g h d", g=2, h=HEADS),
                                v[0][:, two, :, 0:HD], ALU.subtract).then_inc(v_ready, 1)

            def mask_scores(s, j, pair):
                dve.wait_ge(scores_full, 2 * j + pair + 1)
                dve.wait_ge(mask_loaded, 16 * j + 16)
                for g in (0, 1):
                    V.tensor_tensor(sm[:, 2 * pair + g, :, :, :], scores[:, :, g, :, :],
                                    adj_mask[:, 2 * pair + g, :].unsqueeze(1).unsqueeze(1).broadcast_to([128, QT, DT, C]),
                                    ALU.mult).then_inc(sm_ready, 1)

            def row_max(s, j, g):
                dve.wait_ge(sm_ready, G * j + g + 1)
                V.tensor_reduce(mx[:, g, :, :], sm[:, g, :, :, :], AX.X, ALU.max).then_inc(mx_ready, 1)

            def softmax_sums(s, j, g):
                bank = filled(s, f"c{g}")
                heads = bank[:, 0:HEADS * (HD + 1)].rearrange("p (h d) -> p h d", h=HEADS)
                V.reciprocal(rinv[:, g, :], heads[:, :, HD]).then_inc(rinv_ready, 1)

            def context(s, j, g):
                heads = ring[s.bank(f"c{g}")][:, 0:HEADS * (HD + 1)].rearrange("p (h d) -> p h d", h=HEADS)
                dve.wait_ge(rinv_ready, G * j + g + 1)
                V.tensor_tensor(cx[:, g, :].rearrange("p (h d) -> p h d", h=HEADS), heads[:, :, 0:HD],
                                rinv[:, g, :].unsqueeze(2).broadcast_to([128, HEADS, HD]), ALU.mult).then_inc(cx_ready, 1)

            def ct_low(s, j, t):
                low_half(s, f"ct{t}", [a[:, t, :, :].rearrange("p g c -> p (g c)") for a in ct], ct_hi, ct_lo, 2 * j + t + 1)

            def emit(s):
                f, b, p, j = s.front, s.back, s.proj, s.attn
                front, back, proj, attn = (n is not None for n in (f, b, p, j))
                if attn:
                    mask_scores(s, j, 0)
                    row_max(s, j, 0)
                if front:
                    incidence(f)
                if back:
                    hidden_stats(s, b, 0)
                if attn:
                    row_max(s, j, 1)
                if back:
                    hidden_stats(s, b, 1)
                    hidden_stats(s, b, 2)
                    hidden_stats(s, b, 3)
                    hidden_variance(s, b)
                if front:
                    degrees(s, f)
                    reciprocals(s, f)
                if back:
                    scaled_propagator(s, b)
                if back and not later(b):
                    row_constants()
                if attn:
                    mask_scores(s, j, 1)
                    row_max(s, j, 2)
                if back:
                    pr_low(s, b, 0)
                    pr_low(s, b, 1)
                if back and not later(b):
                    centred_weights()
                if attn:
                    row_max(s, j, 3)
                if front:
                    edge_weights(s, f, 0)
                if back:
                    pr_low(s, b, 2)
                    pr_low(s, b, 3)
                if back and not later(b):
                    projections_low()
                if front:
                    second_parts(s, f)
                if back:
                    residual_add(s, b, 0)
                if front:
                    third_parts(s, f)
                if back:
                    residual_stats(b, 0)
                if front:
                    edge_weights(s, f, 1)
                if back:
                    residual_variance(b, 0)
                if front:
                    edge_weights(s, f, 2)
                if back:
                    residual_add(s, b, 1)
                    residual_stats(b, 1)
                if attn:
                    softmax_sums(s, j, 0)
                if back:
                    residual_variance(b, 1)
                if attn:
                    context(s, j, 0)
                if back:
                    normalise(x1_ready, range(0, 2), 2 * b + 1, x1, z1, z1_mv, z1_rstd, z1_rstd_ready)
                if attn:
                    softmax_sums(s, j, 1)
                if back:
                    normalise(x1_ready, range(2, 4), 2 * b + 2, x1, z1, z1_mv, z1_rstd, z1_rstd_ready)
                if attn:
                    context(s, j, 1)
                    softmax_sums(s, j, 2)
                if front and not later(f):
                    biases()
                if front:
                    propagator(s, f)
                if attn:
                    context(s, j, 2)
                if proj:
                    xt_low(s, p, 0)
                    xt_low(s, p, 1)
                if attn:
                    softmax_sums(s, j, 3)
                    context(s, j, 3)
                if front:
                    px_low(s, f, 0)
                if attn:
                    ct_low(s, j, 0)
                    ct_low(s, j, 1)
                    output_residual(s, j, 0)
                    output_residual(s, j, 1)
                    output_stats(j)
                if front:
                    px_low(s, f, 1)
                if attn:
                    output_variance(j)
                if proj:
                    values_low(s, p, 0)
                if attn:
                    dve.wait_ge(stored, 16 * j + 16)
                    normalise(y_ready, range(G), j + 1, y_out, z2, z2_mv, z2_rstd, z2_rstd_ready)
                if proj:
                    values_low(s, p, 1)

            def emit_last(s):
                j = s.attn
                mask_scores(s, j, 0)
                row_max(s, j, 0)
                row_max(s, j, 1)
                mask_scores(s, j, 1)
                row_max(s, j, 2)
                row_max(s, j, 3)
                exponentials_low(j, 0)
                exponentials_low(j, 1)
                softmax_sums(s, j, 0)
                context(s, j, 0)
                exponentials_low(j, 2)
                softmax_sums(s, j, 1)
                context(s, j, 1)
                exponentials_low(j, 3)
                softmax_sums(s, j, 2)
                context(s, j, 2)
                softmax_sums(s, j, 3)
                context(s, j, 3)
                ct_low(s, j, 0)
                ct_low(s, j, 1)
                output_residual(s, j, 0)
                output_residual(s, j, 1)
                output_stats(j)
                output_variance(j)
                dve.wait_ge(stored, 16 * j + 16)
                normalise(y_ready, range(G), j + 1, y_out, z2, z2_mv, z2_rstd, z2_rstd_ready)

            sections(dve, emit, emit_last)

        @block.gpsimd
        def _(pool):
            P = nc.gpsimd
            P.memset(ident_bf[:], 0.0).then_inc(const_ready, 1)
            P.memset(ident[:], 0.0).then_inc(const_ready, 1)
            P.memset(ones_bf[:], 1.0).then_inc(const_ready, 1)
            P.memset(ones_r[:].bitcast(F32), 1.0).then_inc(const_ready, 1)
            P.memset(mean_w[:], 1.0 / DH).then_inc(const_ready, 1)
            P.memset(neg_half[:], -0.5).then_inc(const_ready, 1)
            P.memset(half[:], 0.5).then_inc(const_ready, 1)
            P.memset(p_bias[:], P_SCALE_LOG2 * math.log(2.0)).then_inc(const_ready, 1)
            pool.wait_ge(const_ready, 8)
            for m in (ident_bf, ident):
                P.affine_select(out=m[:], in_=m[:], compare_op=ALU.not_equal, fill=1.0, base=0,
                                pattern=[[-1, 128]], channel_multiplier=1).then_inc(const_ready, 1)
            pool.sem_inc(stored, 16)

            pool.wait_ge(w1_hi, 1)
            P.tensor_tensor(W1[1][:].rearrange("p t n -> p (t n)"), w1_in,
                            W1[0][:].rearrange("p t n -> p (t n)").bitcast(F32), ALU.subtract).then_inc(w1_ready, 1)
            pool.wait_ge(vectors_loaded, 32)
            pool.wait_ge(w2_loaded, 16)
            for t in range(HT_):
                P.tensor_scalar(w2_gamma[:, t * D:(t + 1) * D], w2_in[:, t * D:(t + 1) * D], gamma_cols[:, t:t + 1], 0.0,
                                ALU.mult, ALU.add).then_inc(products_in, 1)
            pool.wait_ge(proj_loaded, 16)
            P.tensor_tensor(v_squares, proj_in[:, 2, :], proj_in[:, 2, :], ALU.mult).then_inc(products_in, 1)
            P.tensor_scalar(proj_in[:, 0, :], proj_in[:, 0, :], QSCALE, 0.0, ALU.mult, ALU.add).then_inc(proj_scaled, 1)

            def scale_values():
                pool.wait_ge(norm_ready, 1)
                P.tensor_tensor(v_norm[:, 2:3], v_norm[:, 1:2], neg_half[:, 0:1], ALU.pow).then_inc(v_scale_ready, 1)
                P.tensor_tensor(v_norm[:, 3:4], v_norm[:, 1:2], half[:], ALU.pow).then_inc(v_scale_ready, 1)
                pool.wait_ge(v_scale_ready, 2)
                P.tensor_scalar(proj_in[:, 2, :], proj_in[:, 2, :], v_norm[:, 2:3], V_SCALE,
                                ALU.mult, ALU.mult).then_inc(proj_scaled, 1)
                P.tensor_scalar(proj_in[:, 3, :], proj_in[:, 3, :], v_norm[:, 3:4], 1.0 / V_SCALE,
                                ALU.mult, ALU.mult).then_inc(proj_scaled, 1)

            def inverse_root(rstd, var, ready):
                P.tensor_tensor(rstd, var, neg_half[:, 0:var.shape[1]], ALU.pow).then_inc(ready, 1)

            def residual1(s, i):
                pool.wait_ge(x_loaded, 16 * i + 16)
                pool.wait_ge(cols_step, COLS_STEPS * i + COLS_STEPS)
                P.tensor_tensor(res1_b[:], x_in[:], x_in[:], ALU.add).then_inc(res1_step, 1)
                if not later(i):
                    pool.wait_ge(rows_ready, 2)
                for g in range(G):
                    last = P.tensor_scalar(res1[:, g, :], u_rows[:], rs[:, g:g + 1], 0.0, ALU.mult, ALU.add)
                last.then_inc(res1_step, 1)
                pool.wait_ge(res1_step, 4 * i + 1)
                P.tensor_tensor(res1_b[:], res1_b[:], b2_rows.unsqueeze(1).broadcast_to([128, G, D]),
                                ALU.add).then_inc(res1_step, 1)
                pool.wait_ge(res1_step, 4 * i + 3)
                P.tensor_tensor(res1[:], res1[:], res1_b[:], ALU.add).then_inc(res1_step, 1)

            def residual2(s, j, again):
                if again:
                    pool.wait_ge(z2_ready, 2 * j)
                pool.wait_ge(x1_ready, G * j + G)
                P.tensor_tensor(res2[:], x1[:], bo_rows.unsqueeze(1).broadcast_to([128, G, D]),
                                ALU.add).then_inc(res2_ready, 1)

            def subtract_max(s, j, g):
                pool.wait_ge(mx_ready, G * j + g + 1)
                P.tensor_tensor(sm[:, g, :, :, :], sm[:, g, :, :, :],
                                mx[:, g, :, :].unsqueeze(3).broadcast_to([128, QT, DT, C]), ALU.subtract).then_inc(sub_ready, 1)

            def exponentials_low(j, g):
                pool.wait_ge(p_all, DT * (G * j + g + 1))
                P.tensor_tensor(pT[1][:, g, :, :], p_full[:, g, :, :], pT[0][:, g, :, :], ALU.subtract).then_inc(p_lo, 1)

            def emit(s):
                f, b, p, j = s.front, s.back, s.proj, s.attn
                front, back, proj, attn = (n is not None for n in (f, b, p, j))
                if attn:
                    subtract_max(s, j, 0)
                    subtract_max(s, j, 1)
                if back:
                    pool.wait_ge(r_var_ready, b + 1)
                    inverse_root(r_rstd[:], r_var[:], r_rstd_ready)
                if back and not later(b):
                    residual1(s, b)
                    scale_values()
                if attn:
                    exponentials_low(j, 0)
                    subtract_max(s, j, 2)
                    subtract_max(s, j, 3)
                    exponentials_low(j, 1)
                if back:
                    pool.wait_ge(z1_var_ready, 2 * b + 1)
                    inverse_root(z1_rstd[:, 0:2], z1_var[:, 0:2], z1_rstd_ready)
                if attn:
                    exponentials_low(j, 2)
                if back:
                    pool.wait_ge(z1_var_ready, 2 * b + 2)
                    inverse_root(z1_rstd[:, 2:4], z1_var[:, 2:4], z1_rstd_ready)
                if attn:
                    exponentials_low(j, 3)
                if front and later(f):
                    residual1(s, f)
                if attn:
                    pool.wait_ge(z2_var_ready, j + 1)
                    inverse_root(z2_rstd[:], z2_var[:], z2_rstd_ready)
                if proj:
                    residual2(s, p, attn)

            def emit_last(s):
                j = s.attn
                subtract_max(s, j, 0)
                subtract_max(s, j, 1)
                subtract_max(s, j, 2)
                subtract_max(s, j, 3)
                pool.wait_ge(z2_var_ready, j + 1)
                inverse_root(z2_rstd[:], z2_var[:], z2_rstd_ready)

            sections(pool, emit, emit_last)


_OUTS = [((128, 128, 256), 'float32')]


def kernel(**inputs):
    import numpy as _np
    import concourse.bacc as _bacc
    from concourse import mybir as _mybir
    from concourse.bass_utils import run_bass_kernel_spmd as _run

    nc = _bacc.Bacc("TRN2", target_bir_lowering=False, num_devices=1)
    p = {k.replace("L0_gnn_", "").replace("L1_gnn_", ""): _np.asarray(v) for k, v in inputs.items()}
    def columns(a):
        return a.reshape(-1, 128).T

    order = [("x", p["x"]), ("adj", p["adj"]), ("w1t", p["W1"].T), ("w2t", p["W2"].T),
             ("w_proj", _np.stack([p[m].T for m in ("Wq", "Wk", "Wv", "Wo")])), ("b1", p["b1"]),
             ("vec_cols", _np.concatenate([columns(p[v]) for v in ("bq", "bk", "bv", "gamma", "beta")], axis=1)),
             ("vec_rows", _np.concatenate([p["b2"], p["bo"]]))]
    arrays, args = {}, []
    for name, a in order:
        a = _np.ascontiguousarray(a)
        arrays[f"in_{name}"] = a
        args.append(nc.dram_tensor(f"in_{name}", a.shape, _mybir.dt.from_np(a.dtype), kind="ExternalInput").ap())
    for i, (shape, dtype) in enumerate(_OUTS):
        args.append(nc.dram_tensor(f"out_{i}_dram", shape, _mybir.dt.from_np(_np.dtype(dtype)), kind="ExternalOutput").ap())
    gnn_kernel(nc, *args)
    r = _run(nc, [arrays], core_ids=[0])
    return r.results[0]["out_0_dram"]
```
